# Optimizing a Trainium2 kernel written in Bass

```python
import numpy as np
import jax
import jax.numpy as jnp

def _softmax(x, axis=-1):
    return jax.nn.softmax(x, axis=axis)

def _gelu(x):
    return jax.nn.gelu(x, approximate=True)

def _silu(x):
    return jax.nn.silu(x)

def _sigmoid(x):
    return jax.nn.sigmoid(x)

def _layernorm(x, axis=-1, eps=1e-05):
    m = jnp.mean(x, axis=axis, keepdims=True)
    v = jnp.var(x, axis=axis, keepdims=True)
    return (x - m) / jnp.sqrt(v + eps)

def _scatter_add(tgt, idx, src, axis=0):
    return tgt.at[idx].add(src)

def _segment_sum(src, seg, n):
    return jax.ops.segment_sum(src, seg, n)
kernel_name = 'mk_decoder_preln_d1_seqx_r8_1d733e'

def setup_inputs(seed: int=0):
    np.random.seed(seed)
    _w = jnp.asarray

    def _rec_inputs():
        import jax
        import jax.numpy as jnp
        _rk = jax.random.key(seed)
        x = 7.22e-05 + 1 * jax.random.normal(jax.random.fold_in(_rk, 1), (32, 128, 128), jnp.float32)
        _lenS = 128 - jax.random.randint(jax.random.fold_in(_rk, 7), (32,), 0, max(1, 128 // 4) + 1, jnp.int32)
        _lenS2 = 128 - jax.random.randint(jax.random.fold_in(_rk, 8), (32,), 0, max(1, 128 // 4) + 1, jnp.int32)
        _ctx_1024P = jax.random.normal(jax.random.fold_in(_rk, 11), (32, 16, 128), jnp.float32)
        _ctx_1024c = jax.random.dirichlet(jax.random.fold_in(_rk, 511), 0.3 * jnp.ones((16,), jnp.float32), (32, 128))
        _ctx_1024t = jnp.einsum('bsk,bkd->bsd', _ctx_1024c, _ctx_1024P)
        _ctx_1024t = _ctx_1024t * jax.lax.rsqrt(jnp.mean(jnp.square(_ctx_1024t)) + 1e-12) * 0.953939
        ctx_1024 = 4.13588e-05 + 0.999923 * (_ctx_1024t + 0.3 * jax.random.normal(jax.random.fold_in(_rk, 611), (32, 128, 128), jnp.float32))
        return (x, ctx_1024)
    x, ctx_1024 = _rec_inputs()

    def _L0_attn_setup():
        import jax, jax.numpy as jnp
        import numpy as np
        B, T, C, R = (8, 128, 128, 64)
        EPS = 1e-05
        key = jax.random.key(seed)
        ks = jax.random.split(key, 8)
        x = jax.random.normal(ks[0], (B, T, C), dtype=jnp.float32)
        W_attn = jax.random.normal(ks[1], (3 * C, C), dtype=jnp.float32) * 0.02
        W_proj = jax.random.normal(ks[2], (C, C), dtype=jnp.float32) * 0.02
        lora_attn_A = jax.random.normal(ks[3], (C, R), dtype=jnp.float32) * 0.02
        lora_attn_B = jax.random.normal(ks[4], (R, 3 * C), dtype=jnp.float32) * 0.02
        lora_proj_A = jax.random.normal(ks[5], (C, R), dtype=jnp.float32) * 0.02
        lora_proj_B = jax.random.normal(ks[6], (R, C), dtype=jnp.float32) * 0.02
        bn_gamma = jnp.ones((3 * C,), dtype=jnp.float32)
        bn_beta = jnp.zeros((3 * C,), dtype=jnp.float32)
        return {'x': x, 'W_attn': W_attn, 'W_proj': W_proj, 'lora_attn_A': lora_attn_A, 'lora_attn_B': lora_attn_B, 'lora_proj_A': lora_proj_A, 'lora_proj_B': lora_proj_B, 'bn_gamma': bn_gamma, 'bn_beta': bn_beta}
    _L0_attn_all = _L0_attn_setup()
    _L0_attn_in = {k: v for k, v in _L0_attn_all.items() if k in ('W_attn', 'W_proj', 'lora_attn_A', 'lora_attn_B', 'lora_proj_A', 'lora_proj_B', 'bn_gamma', 'bn_beta')}
    del _L0_attn_all

    def _L0_xattn_setup():
        import jax, jax.numpy as jnp
        import numpy as np
        D_MODEL = 128
        HEADS = 16
        D_HEAD = D_MODEL // HEADS
        SEQ = 256
        C = 2
        K_TOP = int(C * np.log(SEQ))
        key = jax.random.key(seed)
        ks = jax.random.split(key, 5)
        s = 0.02
        return {'Q': jax.random.normal(ks[0], (4, SEQ, D_MODEL), jnp.float32), 'K': jax.random.normal(ks[1], (4, SEQ, D_MODEL), jnp.float32), 'V': jax.random.normal(ks[2], (4, SEQ, D_MODEL), jnp.float32), 'Wq': jax.random.normal(ks[3], (D_MODEL, D_HEAD), jnp.float32) * s, 'bq': jnp.zeros((D_HEAD,), jnp.float32), 'Wout': jax.random.normal(ks[4], (HEADS * D_HEAD, D_MODEL), jnp.float32) * s, 'bout': jnp.zeros((D_MODEL,), jnp.float32)}
    _L0_xattn_all = _L0_xattn_setup()
    _L0_xattn_in = {k: v for k, v in _L0_xattn_all.items() if k in ('Wq', 'bq', 'Wout', 'bout')}
    del _L0_xattn_all

    def _L0_ffn_setup():
        import jax, jax.numpy as jnp
        import numpy as np
        B, S, D_MODEL, D_FF = (4, 256, 128, 512)

        def _quantum_transform(hidden, theta, w_real, w_imag):
            imag = w_imag * jnp.sin(theta + hidden * 0.1)
            quantum_phase = jnp.cos(theta) * w_real + jnp.sin(theta) * w_imag
            return hidden + quantum_phase * imag * 0.1
        key = jax.random.key(seed)
        ks = jax.random.split(key, 8)
        return {'x': jax.random.normal(ks[0], (B, S, D_MODEL), dtype=jnp.float32), 'W1': jax.random.normal(ks[1], (D_MODEL, D_FF), dtype=jnp.float32) * (1.0 / np.sqrt(D_MODEL)), 'b1': jnp.zeros((D_FF,), dtype=jnp.float32), 'quantum_phases': jax.random.normal(ks[2], (D_FF,), dtype=jnp.float32) * (2.0 * np.pi), 'quantum_weights_real': jax.random.normal(ks[3], (D_FF,), dtype=jnp.float32) * 0.1, 'quantum_weights_imag': jax.random.normal(ks[4], (D_FF,), dtype=jnp.float32) * 0.1, 'W2': jax.random.normal(ks[5], (D_FF, D_MODEL), dtype=jnp.float32) * (1.0 / np.sqrt(D_FF)), 'b2': jnp.zeros((D_MODEL,), dtype=jnp.float32)}
    _L0_ffn_all = _L0_ffn_setup()
    _L0_ffn_in = {k: v for k, v in _L0_ffn_all.items() if k in ('W1', 'b1', 'quantum_phases', 'quantum_weights_real', 'quantum_weights_imag', 'W2', 'b2')}
    del _L0_ffn_all
    return {'x': x, 'ctx_1024': ctx_1024, 'L0_attn_W_attn': _L0_attn_in['W_attn'], 'L0_attn_W_proj': _L0_attn_in['W_proj'], 'L0_attn_lora_attn_A': _L0_attn_in['lora_attn_A'], 'L0_attn_lora_attn_B': _L0_attn_in['lora_attn_B'], 'L0_attn_lora_proj_A': _L0_attn_in['lora_proj_A'], 'L0_attn_lora_proj_B': _L0_attn_in['lora_proj_B'], 'L0_attn_bn_gamma': _L0_attn_in['bn_gamma'], 'L0_attn_bn_beta': _L0_attn_in['bn_beta'], 'L0_xattn_Wq': _L0_xattn_in['Wq'], 'L0_xattn_bq': _L0_xattn_in['bq'], 'L0_xattn_Wout': _L0_xattn_in['Wout'], 'L0_xattn_bout': _L0_xattn_in['bout'], 'L0_ffn_W1': _L0_ffn_in['W1'], 'L0_ffn_b1': _L0_ffn_in['b1'], 'L0_ffn_quantum_phases': _L0_ffn_in['quantum_phases'], 'L0_ffn_quantum_weights_real': _L0_ffn_in['quantum_weights_real'], 'L0_ffn_quantum_weights_imag': _L0_ffn_in['quantum_weights_imag'], 'L0_ffn_W2': _L0_ffn_in['W2'], 'L0_ffn_b2': _L0_ffn_in['b2']}

def reference(x, ctx_1024, L0_attn_W_attn, L0_attn_W_proj, L0_attn_lora_attn_A, L0_attn_lora_attn_B, L0_attn_lora_proj_A, L0_attn_lora_proj_B, L0_attn_bn_gamma, L0_attn_bn_beta, L0_xattn_Wq, L0_xattn_bq, L0_xattn_Wout, L0_xattn_bout, L0_ffn_W1, L0_ffn_b1, L0_ffn_quantum_phases, L0_ffn_quantum_weights_real, L0_ffn_quantum_weights_imag, L0_ffn_W2, L0_ffn_b2):
    import jax
    import jax.numpy as jnp

    def _L0_attn_ref(x, W_attn, W_proj, lora_attn_A, lora_attn_B, lora_proj_A, lora_proj_B, bn_gamma, bn_beta):
        import jax, jax.numpy as jnp
        import numpy as np
        B, T, C, R = (8, 128, 128, 64)
        EPS = 1e-05
        Bb, Tt, Cc = x.shape
        Wm_attn = W_attn + (lora_attn_A @ lora_attn_B).reshape(W_attn.shape)
        xa = jnp.einsum('btc,dc->btd', x, Wm_attn)
        mean = xa.mean(axis=(0, 1))
        var = xa.var(axis=(0, 1))
        xa = (xa - mean) * jax.lax.rsqrt(var + EPS) * bn_gamma + bn_beta
        q, k, v = jnp.split(xa, 3, axis=-1)
        scale = 1.0 / jnp.sqrt(jnp.asarray(Cc, dtype=x.dtype))
        att = jnp.einsum('btc,bsc->bts', q, k) * scale
        causal = jnp.tril(jnp.ones((Tt, Tt), dtype=bool))
        att = jnp.where(causal[None, :, :], att, -jnp.inf)
        att = jax.nn.softmax(att, axis=-1)
        y = jnp.einsum('bts,bsc->btc', att, v)
        y = jnp.einsum('btc,dc->btd', y, W_proj)
        Wm_proj = W_proj + (lora_proj_A @ lora_proj_B).reshape(W_proj.shape)
        y = jnp.einsum('btc,dc->btd', y, Wm_proj)
        return y

    def _L0_xattn_ref(Q, K, V, Wq, bq, Wout, bout):
        import jax, jax.numpy as jnp
        import numpy as np
        D_MODEL = 128
        HEADS = 16
        D_HEAD = D_MODEL // HEADS
        SEQ = 256
        C = 2
        K_TOP = int(C * np.log(SEQ))
        B, L, _ = Q.shape
        q = (Q @ Wq + bq).transpose(0, 2, 1)
        k_ = (K @ Wq + bq).transpose(0, 2, 1)
        v = (V @ Wq + bq).transpose(0, 2, 1)
        Qf = jnp.fft.fft(q.astype(jnp.complex64))
        Kf = jnp.fft.fft(k_.astype(jnp.complex64))
        corr = jnp.real(jnp.fft.ifft(Qf * jnp.conj(Kf)))
        corr = corr.mean(axis=(0, 1))
        W_topk, I_topk = jax.lax.top_k(corr, K_TOP)
        W_topk = jax.nn.softmax(W_topk)

        def body(R, ws):
            w, shift = ws
            return (R + w * jnp.roll(v, -shift, axis=-1), None)
        R3, _ = jax.lax.scan(body, jnp.zeros_like(v), (W_topk, I_topk))
        R = jnp.broadcast_to(R3[:, None], (B, HEADS, D_HEAD, L)).reshape(B, L, HEADS * D_HEAD)
        return R @ Wout + bout

    def _L0_ffn_ref(x, W1, b1, quantum_phases, quantum_weights_real, quantum_weights_imag, W2, b2):
        import jax, jax.numpy as jnp
        import numpy as np
        B, S, D_MODEL, D_FF = (4, 256, 128, 512)

        def _quantum_transform(hidden, theta, w_real, w_imag):
            imag = w_imag * jnp.sin(theta + hidden * 0.1)
            quantum_phase = jnp.cos(theta) * w_real + jnp.sin(theta) * w_imag
            return hidden + quantum_phase * imag * 0.1
        hidden = jnp.einsum('bsd,df->bsf', x, W1) + b1
        q = _quantum_transform(hidden, quantum_phases, quantum_weights_real, quantum_weights_imag)
        act = jax.nn.relu(q)
        return jnp.einsum('bsf,fd->bsd', act, W2) + b2
    x = x + _L0_attn_ref(_layernorm(x, axis=-1), L0_attn_W_attn, L0_attn_W_proj, L0_attn_lora_attn_A, L0_attn_lora_attn_B, L0_attn_lora_proj_A, L0_attn_lora_proj_B, L0_attn_bn_gamma, L0_attn_bn_beta)
    x = x + _L0_xattn_ref(_layernorm(x, axis=-1), ctx_1024, ctx_1024, L0_xattn_Wq, L0_xattn_bq, L0_xattn_Wout, L0_xattn_bout)
    x = x + _L0_ffn_ref(_layernorm(x, axis=-1), L0_ffn_W1, L0_ffn_b1, L0_ffn_quantum_phases, L0_ffn_quantum_weights_real, L0_ffn_quantum_weights_imag, L0_ffn_W2, L0_ffn_b2)
    return x

_drawn_inputs = setup_inputs


def setup_inputs(seed=0):
    import zlib

    import numpy as np

    out = dict(_drawn_inputs(seed))
    spreads = {'L0_attn_bn_gamma': (1.0, 0.6),
     'L0_attn_bn_beta': (0.0, 0.8),
     'L0_xattn_bq': (0.0, 0.541),
     'L0_xattn_bout': (0.0, 0.1),
     'L0_ffn_b1': (0.0, 0.332),
     'L0_ffn_b2': (0.0, 0.1)}
    factors = {'L0_attn_W_attn': 3.584,
     'L0_attn_W_proj': 3.335,
     'L0_attn_lora_attn_A': 8.0,
     'L0_attn_lora_attn_B': 8.0,
     'L0_attn_lora_proj_A': 8.0,
     'L0_attn_lora_proj_B': 8.0,
     'L0_ffn_quantum_phases': 33.917,
     'L0_ffn_quantum_weights_real': 60.145,
     'L0_ffn_quantum_weights_imag': 24.792,
     'ctx_1024': 4.603,
     'L0_xattn_Wq': 4.575,
     'L0_xattn_Wout': 2.77}
    for name, (base, spread) in spreads.items():
        noise = np.random.default_rng([zlib.crc32(name.encode()), seed]).standard_normal(out[name].shape)
        drawn = base * np.exp(spread * noise) if base else spread * noise
        out[name] = jnp.asarray(drawn.astype(out[name].dtype))
    for name, factor in factors.items():
        out[name] = (out[name] * factor).astype(out[name].dtype)
    return out
```

```python
import math
from contextlib import ExitStack

import numpy as np
import concourse.bass as bass
from concourse import mybir

FP32 = mybir.dt.float32
BF16 = mybir.dt.bfloat16
INT32 = mybir.dt.int32
ALU = mybir.AluOpType
ACT = mybir.ActivationFunctionType
AX = mybir.AxisListType

B, T, C = 32, 128, 128
G = 4
NG = B // G
W = G * T
RANK = 64
HD = 8
BH = B * HD
F = 512
FC = F // 128
EPS = 1e-5
K_TOP = int(2 * math.log(256))
TWO_PI = 2.0 * math.pi
PI_A = 6.28125
PI_B = float(np.float32(np.round((TWO_PI - PI_A) * 2**21) / 2**21))
PI_C = TWO_PI - PI_A - PI_B
ROUND = 1.5 * 2.0**23
INSIDE = 1.0 - 1e-6
MASKED = -1e30
PADDING, TAKEN = -2e38, -3e38
NV = 18
V_GAMMA, V_BETA, V_THETA, V_REAL, V_IMAG = 0, 3, 6, 10, 14
R_BOUT, R_B2, R_BQ, R_B1 = 0, C, 2 * C, 2 * C + HD
NR = R_B1 + F
LAG = 4
NCH = NG * FC
HB, OB = (1, 2, 3, 6), (5, 7)
NACT = 6
(T_TURN, T_ANGLE, T_ROUND, T_RED, T_SIN, T_SINH, T_COS, T_MIX, T_KAPPA) = range(9)


def decoder_layer(nc, x, ctx_in, w_attn, w_proj, a_attn, b_attn, a_proj, b_proj, gamma, beta,
                  wq, bq, wout, bout, w1, b1, theta, w_real, w_imag, w2, b2, cos_t, sin_t, out):
    es = ExitStack()
    with es:
        def sb(name, shape, dt=FP32):
            return es.enter_context(nc.sbuf_tensor(name, shape, dt))

        def sem(name):
            return es.enter_context(nc.semaphore(name))

        xs = sb("xs", [T, B, C])
        cs = sb("cs", [T, B, C])
        xn = sb("xn", [T, B, C + 1])
        xnT = sb("xnT", [C, B, T])
        cT = sb("cT", [C, 2, W])
        ident = sb("ident", [128, 128])
        identb = sb("identb", [128, 128], BF16)
        maskb = sb("maskb", [T, T], BF16)
        cosm = sb("cosm", [T, T])
        sinm = sb("sinm", [T, T])
        ones = sb("ones", [128, 128])
        half = sb("half", [128, B])
        vrow = sb("vrow", [NV, 128])
        vcol = sb("vcol", [128, NV])
        rrow = sb("rrow", [1, NR])
        inv128 = sb("inv128", [1, 128])
        negmean = sb("negmean", [128, 128])
        bc = sb("bc", [128, R_B1])
        wa = sb("wa", [128, 3, C])
        lo_a = sb("lo_a", [128, RANK])
        lo_b = sb("lo_b", [RANK, 3 * C])
        lp_a = sb("lp_a", [128, RANK])
        lp_b = sb("lp_b", [RANK, C])
        spread = sb("spread", [RANK, 3, 3 * C])
        lp_aT = sb("lp_aT", [RANK, 128])
        wp = sb("wp", [C, C])
        wmpT = sb("wmpT", [C, C])
        woT = sb("woT", [C, C])
        wm = sb("wm", [128, 3, C])
        wsum = sb("wsum", [128, 3])
        wmT = sb("wmT", [C, 3, C])
        gram = sb("gram", [C, C + 1])
        tg = sb("tg", [C, 3, C])
        q2 = sb("q2", [128, 3])
        mu = sb("mu", [128, 3])
        bn = sb("bn", [128, 6, 3])
        w3 = sb("w3", [128, 3, C])
        mqk = sb("mqk", [C, C])
        wvo = sb("wvo", [C, C])
        st = sb("st", [T, B, 6])
        mv = sb("mv", [T, B, 2])
        ve = sb("ve", [T, B])
        rstd = sb("rstd", [T, B])
        mr = sb("mr", [T, B])
        shift = sb("shift", [T, B])
        gT = sb("gT", [C, 2, W])
        p = sb("p", [T, 2, G, T])
        negmax = sb("negmax", [T, B])
        rowsum = sb("rowsum", [T, B])
        rinv = sb("rinv", [T, B])
        pT = sb("pT", [T, 2, W])
        yT = sb("yT", [C, 2, W])
        ln = sb("ln", [T, 2, G, C])
        lnT = sb("lnT", [C, 2, W])
        wqs = sb("wqs", [C, HD])
        wouts = sb("wouts", [T, C])
        kv = sb("kv", [T, BH])
        q = sb("q", [T, BH])
        kh = sb("kh", [T, 2, BH])
        kx = sb("kx", [T, 2, BH])
        junk = sb("junk", [128, 512])
        junk2 = sb("junk2", [128, 512])
        pw = sb("pw", [T, 2])
        pwb = sb("pwb", [T, 2, T])
        cw = sb("cw", [T, T + 8])
        cw2 = sb("cw2", [T, T + 8])
        cw3 = sb("cw3", [T, T + 8])
        top = sb("top", [T, 16])
        nmx = sb("nmx", [T, 1])
        ex = sb("ex", [T, T])
        sel = sb("sel", [T, T])
        ew = sb("ew", [T, T])
        wsm = sb("wsm", [T, 6])
        wf = sb("wf", [T, 2, C])
        ab = sb("ab", [T, 4, C])
        z = sb("z", [T, C])
        w1s = sb("w1s", [C, F])
        w1p = sb("w1p", [C, F])
        w2s = sb("w2s", [128, FC, C])
        th = sb("th", [128, 9, FC])
        turn = sb("turn", [128, 2, W], INT32)
        ang = sb("ang", [128, 2, W])
        sn = sb("sn", [128, 2, W])
        hid = sb("hid", [128, 2, W])
        act_f = sb("act_f", [128, NACT, W])
        outs = sb("outs", [T, 2, G, C])

        bank = [es.enter_context(nc.psum_tensor(f"bank{i}", [128, 512], FP32)) for i in range(8)]

        x_in = [sem(f"x_in{g}") for g in range(NG)]
        c_in = [sem(f"c_in{g}") for g in range(NG)]
        attn_w_in, vec_in, proj_w_in, cross_w_in, dft_in, w1_in, w2_in = (
            sem(n) for n in ("attn_w_in", "vec_in", "proj_w_in", "cross_w_in", "dft_in", "w1_in", "w2_in"))
        out_sent = [sem("out_sent0"), sem("out_sent1")]
        (consts_set, small_tposed, lora_spread, vec_copied, lora_prod, wm_ready, wm_tposed, wmT_copied,
         wmpT_done, wmpT_copied, woT_done, woT_copied, bias_spread, bias_copied, gram_done, gram_copied,
         tg_done, bn_var, bn_rstd, w3_ready, mqk_done, mqk_copied, wf_done, wf_copied, kv_ready, kspec_done,
         kspec_copied, w1_mean, w1_ready, theta_ready, sines_done, kappa_ready, q_ready, qspec_done,
         power_ready, corr_done, corr_copied, top_ready, lag_exp, zspec_ready, z_done, z_copied) = (
            sem(n) for n in (
                "consts_set", "small_tposed", "lora_spread", "vec_copied", "lora_prod", "wm_ready", "wm_tposed",
                "wmT_copied", "wmpT_done", "wmpT_copied", "woT_done", "woT_copied", "bias_spread", "bias_copied",
                "gram_done", "gram_copied", "tg_done", "bn_var", "bn_rstd", "w3_ready", "mqk_done", "mqk_copied",
                "wf_done", "wf_copied", "kv_ready", "kspec_done", "kspec_copied", "w1_mean", "w1_ready",
                "theta_ready", "sines_done", "kappa_ready", "q_ready", "qspec_done", "power_ready", "corr_done",
                "corr_copied", "top_ready", "lag_exp", "zspec_ready", "z_done", "z_copied"))
        pool_seq = sem("pool_seq")
        dve_seq = sem("dve_seq")
        stats = sem("stats")
        scaled = sem("scaled")
        normed = sem("normed")
        tposed = sem("tposed")
        tcopied = sem("tcopied")
        resid = sem("resid")
        biased = sem("biased")
        (ct_done, ct_copied, k_done, g_done, g_copied, s_done, max_done, pt_done, pt_copied, yt_done, yt_copied,
         y_done, q_done, r_done, o_done) = (
            sem(n) for n in ("ct_done", "ct_copied", "k_done", "g_done", "g_copied", "s_done", "max_done",
                             "pt_done", "pt_copied", "yt_done", "yt_copied", "y_done", "q_done", "r_done", "o_done"))
        v_repeated = sem("v_repeated")
        exp_done = sem("exp_done")
        h_done, turn_done, ang_done, sin_done, hid_done, relu_done, down_done = (
            sem(n) for n in ("h_done", "turn_done", "ang_done", "sin_done", "hid_done", "relu_done", "down_done"))

        block = es.enter_context(nc.Block())

        def grp(t, g):
            return t[:, g * G:(g + 1) * G, :]

        def flat(ap):
            return ap.rearrange("p a b -> p (a b)")

        @block.sync
        def _(sp):
            for g in range(NG):
                sp.dma_start(grp(xs, g), x[g * G:(g + 1) * G].rearrange("b t c -> t b c")).then_inc(x_in[g], 16)
            for g in range(NG):
                sp.dma_start(grp(cs, g), ctx_in[g * G:(g + 1) * G].rearrange("b t c -> t b c")).then_inc(c_in[g], 16)
            sp.dma_start(w1s[:, :], w1).then_inc(w1_in, 16)
            sp.dma_start(rrow[0:1, R_B1:NR], b1.unsqueeze(0)).then_inc(w1_in, 16)
            sp.dma_start(w2s[:, :, :], w2.rearrange("(f p) d -> p f d", p=128)).then_inc(w2_in, 16)
            for g in range(NG):
                sp.wait_ge(o_done, g + 1)
                sp.dma_start(out[g * G:(g + 1) * G].rearrange("b t c -> t b c"),
                             outs[:, g % 2, :, :]).then_inc(out_sent[g % 2], 16)
            sp.wait_ge(out_sent[0], 16 * (NG // 2))
            sp.wait_ge(out_sent[1], 16 * (NG // 2))

        @block.gpsimd
        def _(pool):
            seq = [0]

            def after(ins):
                seq[0] += 1
                ins.then_inc(pool_seq, 1)
                pool.wait_ge(pool_seq, seq[0])

            pool.memset(ident[:, :], 0.0).then_inc(pool_seq, 1)
            pool.memset(maskb[:, :], 0.0).then_inc(pool_seq, 1)
            seq[0] += 2
            pool.wait_ge(pool_seq, seq[0])
            after(pool.affine_select(out=ident[:, :], in_=ident[:, :], compare_op=ALU.not_equal, fill=1.0,
                                     base=0, pattern=[[-1, 128]], channel_multiplier=1))
            pool.affine_select(out=maskb[:, :], in_=maskb[:, :], compare_op=ALU.is_ge, fill=MASKED,
                               base=0, pattern=[[-1, 128]], channel_multiplier=1).then_inc(consts_set, 1)
            pool.tensor_copy(identb[:, :], ident[:, :]).then_inc(consts_set, 1)
            pool.memset(ones[:, :], 1.0).then_inc(consts_set, 1)
            pool.memset(inv128[:, :], 1.0 / 128).then_inc(consts_set, 1)
            pool.memset(negmean[:, :], -1.0 / 128).then_inc(consts_set, 1)
            pool.memset(xn[:, :, C:C + 1], 1.0).then_inc(consts_set, 1)
            after(pool.memset(half[:, :], -0.5))

            def scale_group(n, g, add):
                a, b = g * G, (g + 1) * G
                pool.wait_ge(stats, n * NG + g + 1)
                after(pool.tensor_scalar(ve[:, a:b], mv[:, a:b, 1], EPS, 1.0, ALU.add, ALU.mult))
                after(pool.tensor_tensor(rstd[:, a:b], ve[:, a:b], half[:, a:b], ALU.pow))
                after(pool.tensor_tensor(mr[:, a:b], mv[:, a:b, 0], rstd[:, a:b], ALU.mult))
                return pool.tensor_scalar(shift[:, a:b], mr[:, a:b], -1.0, add, ALU.mult, ALU.add)

            def norm_group(n, g, add):
                after(scale_group(n, g, add))
                if g >= 2 or n == 2:
                    pool.wait_ge(tposed, n * NG + g - 1)
                for j in range(G):
                    b = g * G + j
                    ins = pool.tensor_scalar(ln[:, g % 2, j, :], xs[:, b, :], rstd[:, b:b + 1], shift[:, b:b + 1],
                                             ALU.mult, ALU.add)
                ins.then_inc(normed, 1)

            def add_bias(n, g, at):
                pool.wait_ge(normed, n * NG + g + 1)
                row = bc[:, at:at + C].unsqueeze(1).broadcast_to([128, G, C])
                pool.tensor_tensor(grp(xs, g), grp(xs, g), row, ALU.add).then_inc(biased, 1)

            def repeat_v(g):
                pool.wait_ge(kv_ready, 1)
                for j in range(G):
                    b = g * G + j
                    ins = pool.tensor_copy(cs[:, b, :].rearrange("p (r h) -> p r h", h=HD),
                                           kv[:, b * HD:(b + 1) * HD].unsqueeze(1).broadcast_to([T, T // HD, HD]))
                ins.then_inc(v_repeated, 1)

            for g in range(NG):
                scale_group(0, g, 1.0).then_inc(scaled, 1)
            pool.wait_ge(bn_var, 1)
            pool.tensor_tensor(bn[:, 1, :], bn[:, 0, :], half[:, 0:3], ALU.pow).then_inc(bn_rstd, 1)
            pool.wait_ge(bias_copied, 1)
            for g in range(NG):
                norm_group(1, g, 0.0)
                add_bias(1, g, R_BOUT)
                repeat_v(g)

            def relu(k):
                pool.wait_ge(hid_done, k + 1)
                if k >= NACT:
                    pool.wait_ge(down_done, k - NACT + 1)
                pool.tensor_scalar(act_f[:, k % NACT, :], hid[:, k % 2, :], 0.0, None, ALU.max).then_inc(relu_done, 1)

            for g in (0, 1):
                norm_group(2, g, 1.0)
                add_bias(2, g, R_B2)
            for k in range(NCH):
                g, c = divmod(k, FC)
                relu(k)
                if c == 1 and g + 2 < NG:
                    norm_group(2, g + 2, 1.0)
                if c == 2 and g + 2 < NG:
                    add_bias(2, g + 2, R_B2)

        @block.scalar
        def _(act):
            def load(sem_, dst, src):
                act.dma_start(dst, src).then_inc(sem_, 16)

            load(attn_w_in, lo_a[:, :], a_attn)
            load(attn_w_in, lp_a[:, :], a_proj)
            load(attn_w_in, lo_b[:, :], b_attn)
            load(attn_w_in, wa[:, :, :], w_attn.rearrange("(n p) c -> p n c", p=128))
            for at, n, src in ((V_GAMMA, 3, gamma), (V_BETA, 3, beta), (V_THETA, FC, theta),
                               (V_REAL, FC, w_real), (V_IMAG, FC, w_imag)):
                load(vec_in, vrow[at:at + n, :], src.rearrange("(n p) -> n p", p=128))
            load(proj_w_in, wp[:, :], w_proj)
            load(proj_w_in, lp_b[:, :], b_proj)
            load(cross_w_in, wqs[:, :], wq)
            load(cross_w_in, rrow[0:1, R_BOUT:R_BOUT + C], bout.unsqueeze(0))
            load(cross_w_in, rrow[0:1, R_B2:R_B2 + C], b2.unsqueeze(0))
            load(cross_w_in, rrow[0:1, R_BQ:R_BQ + HD], bq.unsqueeze(0))
            load(dft_in, cosm[:, :], cos_t)
            load(dft_in, sinm[:, :], sin_t)
            load(dft_in, wouts[:, :], wout)

            def copy(dst, src, scale=1.0):
                return act.activation(dst, src, ACT.Copy, scale=scale)

            def copy_xT(g):
                act.wait_ge(tposed, g + 1)
                copy(flat(grp(xnT, g)), bank[1 + g % 2][:, :]).then_inc(tcopied, 1)

            def copy_cT(g):
                act.wait_ge(ct_done, g + 1)
                if g >= 2:
                    act.wait_ge(k_done, g - 1)
                copy(cT[:, g % 2, :], bank[3 + g % 2][:, :]).then_inc(ct_copied, 1)

            act.wait_ge(wmpT_done, 1)
            copy(wmpT[:, :], bank[3][:, 0:C]).then_inc(wmpT_copied, 1)
            for g in range(NG):
                copy_xT(g)
                if g == 3:
                    act.wait_ge(wm_tposed, 1)
                    copy(flat(wmT[:, :, :]), bank[7][:, 0:3 * C]).then_inc(wmT_copied, 1)
                if g == 4:
                    act.wait_ge(woT_done, 1)
                    copy(woT[:, :], bank[3][:, C:2 * C]).then_inc(woT_copied, 1)
                if g == 5:
                    act.wait_ge(bias_spread, 1)
                    copy(bc[:, :], bank[7][:, 0:R_B1]).then_inc(bias_copied, 1)
            act.wait_ge(gram_done, 1)
            copy(gram[:, :], bank[0][:, 0:C + 1], scale=1.0 / (B * T)).then_inc(gram_copied, 1)
            for g in range(4):
                copy_cT(g)
            act.wait_ge(theta_ready, 1)
            act.activation(th[:, T_SIN, :], th[:, T_ANGLE, :], ACT.Sin)
            act.activation(th[:, T_SINH, :], th[:, T_ANGLE, :], ACT.Sin, scale=0.5).then_inc(sines_done, 1)
            act.wait_ge(wf_done, 1)
            copy(flat(wf[:, :, :]), bank[7][:, 0:2 * C]).then_inc(wf_copied, 1)
            act.wait_ge(mqk_done, 1)
            copy(mqk[:, :], bank[6][:, 0:C], scale=float(C) ** -0.5)
            copy(wvo[:, :], bank[6][:, C:2 * C]).then_inc(mqk_copied, 1)
            for g in range(4, NG):
                copy_cT(g)

            def copy_g(g):
                act.wait_ge(g_done, g + 1)
                if g >= 2:
                    act.wait_ge(s_done, g - 1)
                copy(gT[:, g % 2, :], bank[1][:, :]).then_inc(g_copied, 1)

            def copy_pT(g):
                act.wait_ge(pt_done, g + 1)
                if g >= 2:
                    act.wait_ge(yt_done, g - 1)
                copy(pT[:, g % 2, :], bank[4][:, :]).then_inc(pt_copied, 1)

            def exps(g, js):
                act.wait_ge(max_done, g + 1)
                if g >= 2:
                    act.wait_ge(pt_done, g - 1)
                for j in js:
                    b = g * G + j
                    act.activation(p[:, g % 2, j, :], bank[2 + g % 2][:, j * T:(j + 1) * T], ACT.Exp,
                                   bias=negmax[:, b:b + 1], accum_out=rowsum[:, b:b + 1]).then_inc(exp_done, 1)

            def copy_lnT(n, g):
                act.wait_ge(tposed, n * NG + g + 1)
                if n == 1 and g >= 2:
                    act.wait_ge(q_done, g - 1)
                if n == 2:
                    act.wait_ge(q_done, NG) if g < 2 else act.wait_ge(h_done, (g - 1) * FC)
                copy(lnT[:, g % 2, :], bank[0][:, :]).then_inc(tcopied, 1)

            copy_g(0)
            for k in range(NG + 3):
                if 1 <= k <= NG:
                    copy_pT(k - 1)
                if k < NG:
                    exps(k, (0, 1))
                if k + 1 < NG:
                    copy_g(k + 1)
                if k < NG:
                    exps(k, (2, 3))
                if 3 <= k:
                    copy_lnT(1, k - 3)

            act.wait_ge(top_ready, 1)
            act.activation(ex[:, :], cw[:, 0:T], ACT.Exp, bias=nmx[:, 0:1]).then_inc(lag_exp, 1)
            act.wait_ge(z_done, 1)
            copy(z[:, :], bank[3][:, 0:C]).then_inc(z_copied, 1)

            def turns(k):
                act.wait_ge(h_done, k + 1)
                if k >= 2:
                    act.wait_ge(ang_done, k - 1)
                act.activation(turn[:, k % 2, :], bank[HB[k % 4]][:, :], ACT.Identity, scale=0.1 / TWO_PI,
                               bias=th[:, T_TURN, k % FC:k % FC + 1]).then_inc(turn_done, 1)

            def sine(k):
                act.wait_ge(ang_done, k + 1)
                if k >= 2:
                    act.wait_ge(hid_done, k - 1)
                act.activation(sn[:, k % 2, :], ang[:, k % 2, :], ACT.Sin, scale=TWO_PI * INSIDE,
                               bias=th[:, T_ANGLE, k % FC:k % FC + 1]).then_inc(sin_done, 1)

            copy_lnT(2, 0)
            for k in range(NCH + 1):
                if k < NCH:
                    turns(k)
                if k:
                    sine(k - 1)
                if k % FC == 2 and k // FC + 1 < NG:
                    copy_lnT(2, k // FC + 1)

        @block.vector
        def _(dve):
            seq = [0]

            def after(ins):
                seq[0] += 1
                ins.then_inc(dve_seq, 1)
                dve.wait_ge(dve_seq, seq[0])

            def copy(dst, src):
                return dve.tensor_copy(dst, src)

            def group_stats(g):
                for j in range(G):
                    ins = dve.bn_stats(st[:, g * G + j, :], xs[:, g * G + j, :])
                after(ins)
                for j in range(G):
                    ins = dve.bn_aggr(mv[:, g * G + j, :], st[:, g * G + j, :])
                ins.then_inc(stats, 1)

            def norm0(g):
                dve.wait_ge(scaled, g + 1)
                for j in range(G):
                    b = g * G + j
                    ins = dve.tensor_scalar(xn[:, b, 0:C], xs[:, b, :], rstd[:, b:b + 1], shift[:, b:b + 1],
                                            ALU.mult, ALU.add)
                ins.then_inc(normed, 1)

            def spread_lora():
                dve.wait_ge(small_tposed, 1)
                for j in range(3):
                    copy(spread[:, j, :].rearrange("r (i k) -> r i k", k=3)[:, :, j], bank[6][0:RANK, 0:128])
                copy(lp_aT[:, :], bank[6][0:RANK, 128:256]).then_inc(lora_spread, 1)
                copy(vcol[:, :], bank[6][:, 256:256 + NV]).then_inc(vec_copied, 1)

            def centre_weights():
                dve.wait_ge(lora_prod, 1)
                after(dve.tensor_tensor(flat(wm[:, :, :]), bank[7][:, 0:3 * C], flat(wa[:, :, :]), ALU.add))
                after(dve.reduce_sum(wsum[:, :], wm[:, :, :], AX.X))
                after(dve.tensor_scalar(wsum[:, :], wsum[:, :], 1.0 / C, None, ALU.mult))
                for n in range(3):
                    ins = dve.tensor_scalar(wm[:, n, :], wm[:, n, :], wsum[:, n:n + 1], None, ALU.subtract)
                ins.then_inc(wm_ready, 1)

            def col(i):
                return th[:, i, :]

            def reduce_theta():
                theta_c = vcol[:, V_THETA:V_THETA + FC]
                dve.wait_ge(vec_copied, 1)
                after(dve.tensor_scalar(col(T_ROUND), theta_c, 1.0 / TWO_PI, ROUND, ALU.mult, ALU.add))
                after(dve.tensor_scalar(col(T_ROUND), col(T_ROUND), ROUND, None, ALU.subtract))
                after(dve.scalar_tensor_tensor(col(T_RED), col(T_ROUND), -PI_A, theta_c, ALU.mult, ALU.add))
                after(dve.scalar_tensor_tensor(col(T_RED), col(T_ROUND), -PI_B, col(T_RED), ALU.mult, ALU.add))
                after(dve.scalar_tensor_tensor(col(T_RED), col(T_ROUND), -PI_C, col(T_RED), ALU.mult, ALU.add))
                dve.tensor_scalar(col(T_TURN), col(T_RED), 1.0 / TWO_PI, None, ALU.mult)
                dve.tensor_scalar(col(T_ANGLE), col(T_RED), INSIDE, None, ALU.mult).then_inc(theta_ready, 1)

            def make_kappa():
                wr, wi = vcol[:, V_REAL:V_REAL + FC], vcol[:, V_IMAG:V_IMAG + FC]
                dve.wait_ge(sines_done, 1)
                after(dve.tensor_tensor(col(T_COS), col(T_SINH), col(T_SINH), ALU.mult))
                after(dve.tensor_scalar(col(T_COS), col(T_COS), -2.0, 1.0, ALU.mult, ALU.add))
                after(dve.tensor_tensor(col(T_COS), col(T_COS), wr, ALU.mult))
                after(dve.tensor_tensor(col(T_MIX), col(T_SIN), wi, ALU.mult))
                after(dve.tensor_tensor(col(T_MIX), col(T_MIX), col(T_COS), ALU.add))
                after(dve.tensor_tensor(col(T_MIX), col(T_MIX), wi, ALU.mult))
                dve.tensor_scalar(col(T_KAPPA), col(T_MIX), 0.1, None, ALU.mult).then_inc(kappa_ready, 1)

            after(dve.memset(spread[:, :, :], 0.0))
            spread_lora()
            for g in range(NG):
                dve.wait_ge(x_in[g], 16)
                group_stats(g)
                if g:
                    norm0(g - 1)
                if g == 1:
                    centre_weights()
                if g == 4:
                    reduce_theta()
            norm0(NG - 1)

            dve.wait_ge(tg_done, 1)
            for n in range(3):
                dve.tensor_tensor(tg[:, n, :], bank[6][:, n * (C + 1):n * (C + 1) + C], wm[:, n, :], ALU.mult)
            after(copy(mu[:, :], bank[6][:, 0:3 * (C + 1)].rearrange("p (n c) -> p n c", n=3)[:, :, C]))
            dve.reduce_sum(q2[:, :], tg[:, :, :], AX.X)
            after(dve.tensor_tensor(bn[:, 2, :], mu[:, :], mu[:, :], ALU.mult))
            dve.scalar_tensor_tensor(bn[:, 0, :], q2[:, :], EPS, bn[:, 2, :], ALU.add,
                                     ALU.subtract).then_inc(bn_var, 1)
            dve.wait_ge(bn_rstd, 1)
            after(dve.tensor_tensor(bn[:, 3, :], bn[:, 1, :], vcol[:, V_GAMMA:V_GAMMA + 3], ALU.mult))
            after(dve.tensor_tensor(bn[:, 4, :], bn[:, 3, :], mu[:, :], ALU.mult))
            after(dve.tensor_tensor(bn[:, 4, :], vcol[:, V_BETA:V_BETA + 3], bn[:, 4, :], ALU.subtract))
            after(dve.tensor_scalar(bn[:, 4, :], bn[:, 4, :], 1.0 / C, None, ALU.mult))
            for n in range(3):
                ins = dve.tensor_scalar(w3[:, n, :], wm[:, n, :], bn[:, 3, n:n + 1], bn[:, 4, n:n + 1],
                                        ALU.mult, ALU.add)
            ins.then_inc(w3_ready, 1)
            make_kappa()

            bqb = bc[:, R_BQ:R_BQ + HD].unsqueeze(1).broadcast_to([128, B, HD])

            def heads(ap):
                return ap.rearrange("p (b h) -> p b h", h=HD)

            dve.wait_ge(k_done, NG)
            dve.wait_ge(bias_copied, 1)
            dve.tensor_tensor(heads(kv[:, :]), heads(bank[5][:, 0:BH]), bqb, ALU.add).then_inc(kv_ready, 1)

            def row_max(g):
                dve.wait_ge(s_done, g + 1)
                dve.tensor_reduce(negmax[:, g * G:(g + 1) * G],
                                  bank[2 + g % 2][:, :].rearrange("p (b t) -> p b t", b=G),
                                  AX.X, ALU.max, negate=True).then_inc(max_done, 1)

            def add_y(g):
                dve.wait_ge(exp_done, (g + 1) * G)
                after(dve.reciprocal(rinv[:, g * G:(g + 1) * G], rowsum[:, g * G:(g + 1) * G]))
                dve.wait_ge(y_done, g + 1)
                for j in range(G):
                    b = g * G + j
                    ins = dve.scalar_tensor_tensor(xs[:, b, :], bank[7][:, j * C:(j + 1) * C], rinv[:, b:b + 1],
                                                   xs[:, b, :], ALU.mult, ALU.add)
                ins.then_inc(resid, 1)

            def copy_yT(g):
                dve.wait_ge(yt_done, g + 1)
                if g >= 2:
                    dve.wait_ge(y_done, g - 1)
                copy(yT[:, g % 2, :], bank[6][:, :]).then_inc(yt_copied, 1)

            for k in range(NG + 2):
                if 2 <= k:
                    add_y(k - 2)
                if k < NG:
                    row_max(k)
                if 2 <= k:
                    dve.wait_ge(resid, k - 1)
                    group_stats(k - 2)
                if 1 <= k <= NG:
                    copy_yT(k - 1)
                if k == 1:
                    dve.wait_ge(kspec_done, 1)
                    copy(flat(kh[:, :, :]), bank[0][:, :])
                    copy(kx[:, 0, :], bank[0][:, BH:2 * BH])
                    dve.tensor_scalar(kx[:, 1, :], bank[0][:, 0:BH], -1.0, None, ALU.mult).then_inc(kspec_copied, 1)
                if k == 2:
                    dve.wait_ge(w1_mean, 1)
                    dve.tensor_tensor(w1p[:, :], bank[0][:, :], w1s[:, :], ALU.add).then_inc(w1_ready, 1)

            dve.wait_ge(q_done, NG)
            dve.tensor_tensor(heads(q[:, :]), heads(bank[5][:, 0:BH]), bqb, ALU.add).then_inc(q_ready, 1)
            dve.wait_ge(qspec_done, 1)
            dve.tensor_tensor_reduce(out=junk[:, :], in0=bank[1][:, :], in1=flat(kh[:, :, :]), scale=1.0, scalar=0.0,
                                     op0=ALU.mult, op1=ALU.add, accum_out=pw[:, 0:1])
            after(dve.tensor_tensor_reduce(out=junk2[:, :], in0=bank[1][:, :], in1=flat(kx[:, :, :]), scale=1.0,
                                           scalar=0.0, op0=ALU.mult, op1=ALU.add, accum_out=pw[:, 1:2]))
            dve.tensor_scalar(pwb[:, 0, :], ones[:, :], pw[:, 0:1], 1.0 / (T * BH), ALU.mult, ALU.mult)
            dve.tensor_scalar(pwb[:, 1, :], ones[:, :], pw[:, 1:2], -1.0 / (T * BH), ALU.mult,
                              ALU.mult).then_inc(power_ready, 1)
            dve.memset(cw[:, T:T + 8], PADDING)
            dve.wait_ge(corr_done, 1)
            copy(cw[:, 0:T], bank[2][:, 0:T]).then_inc(corr_copied, 1)
            dve.wait_ge(corr_copied, 1)
            after(dve.max(top[:, 0:8], cw[:, :]))
            dve.tensor_scalar(nmx[:, :], top[:, 0:1], -1.0, None, ALU.mult).then_inc(top_ready, 1)
            after(dve.match_replace(cw2[:, :], top[:, 0:8], cw[:, :], TAKEN))
            after(dve.max(top[:, 8:16], cw2[:, :]))
            after(dve.memset(top[:, K_TOP:16], PADDING))
            after(dve.match_replace(cw3[:, :], top[:, 8:16], cw2[:, :], TAKEN))
            after(dve.tensor_scalar(sel[:, :], cw3[:, 0:T], TAKEN, None, ALU.is_equal))
            dve.wait_ge(lag_exp, 1)
            after(dve.tensor_tensor_reduce(out=ew[:, :], in0=ex[:, :], in1=sel[:, :], scale=1.0, scalar=0.0,
                                           op0=ALU.mult, op1=ALU.add, accum_out=wsm[:, 0:1]))
            dve.tensor_tensor_reduce(out=junk[:, 0:T], in0=ew[:, :], in1=cosm[:, :], scale=1.0, scalar=0.0,
                                     op0=ALU.mult, op1=ALU.add, accum_out=wsm[:, 1:2])
            dve.tensor_tensor_reduce(out=junk2[:, 0:T], in0=ew[:, :], in1=sinm[:, :], scale=1.0, scalar=0.0,
                                     op0=ALU.mult, op1=ALU.add, accum_out=wsm[:, 2:3])
            after(dve.reciprocal(wsm[:, 3:4], wsm[:, 0:1]))
            after(dve.tensor_scalar(wsm[:, 4:6], wsm[:, 1:3], wsm[:, 3:4], 1.0 / T, ALU.mult, ALU.mult))
            dve.wait_ge(wf_copied, 1)
            dve.tensor_scalar(ab[:, 0, :], wf[:, 1, :], wsm[:, 5:6], None, ALU.mult)
            after(dve.tensor_scalar(ab[:, 1, :], wf[:, 0, :], wsm[:, 5:6], None, ALU.mult))
            dve.scalar_tensor_tensor(ab[:, 2, :], wf[:, 0, :], wsm[:, 4:5], ab[:, 0, :], ALU.mult, ALU.subtract)
            dve.scalar_tensor_tensor(ab[:, 3, :], wf[:, 1, :], wsm[:, 4:5], ab[:, 1, :], ALU.mult,
                                     ALU.add).then_inc(zspec_ready, 1)

            def add_cross(g):
                dve.wait_ge(r_done, g + 1)
                dve.wait_ge(biased, g + 1)
                dve.tensor_tensor(flat(grp(xs, g)), bank[4][:, :], flat(grp(xs, g)), ALU.add).then_inc(resid, 1)
                dve.wait_ge(resid, NG + g + 1)
                group_stats(g)

            def angle(k):
                dve.wait_ge(turn_done, k + 1)
                if k >= 2:
                    dve.wait_ge(sin_done, k - 1)
                dve.scalar_tensor_tensor(ang[:, k % 2, :], bank[HB[k % 4]][:, :], 0.1 / TWO_PI, turn[:, k % 2, :],
                                         ALU.mult, ALU.subtract).then_inc(ang_done, 1)

            def hidden(k):
                dve.wait_ge(sin_done, k + 1)
                if k >= 2:
                    dve.wait_ge(relu_done, k - 1)
                c = k % FC
                dve.scalar_tensor_tensor(hid[:, k % 2, :], sn[:, k % 2, :], th[:, T_KAPPA, c:c + 1],
                                         bank[HB[k % 4]][:, :], ALU.mult, ALU.add).then_inc(hid_done, 1)

            def output(g):
                dve.wait_ge(down_done, (g + 1) * FC)
                dve.wait_ge(biased, NG + g + 1)
                if g >= 2:
                    dve.wait_ge(out_sent[g % 2], 16 * (g // 2))
                dve.tensor_tensor(flat(outs[:, g % 2, :, :]), bank[OB[g % 2]][:, :], flat(grp(xs, g)),
                                  ALU.add).then_inc(o_done, 1)

            dve.wait_ge(kappa_ready, 1)
            add_cross(0)
            add_cross(1)
            for k in range(NCH + LAG + 2):
                if k < NCH:
                    angle(k)
                if 1 <= k <= NCH:
                    hidden(k - 1)
                if k % FC == 0 and k // FC + 2 < NG:
                    add_cross(k // FC + 2)
                if k >= LAG + FC and (k - LAG) % FC == 1:
                    output((k - LAG) // FC - 1)

        @block.tensor
        def _(pe):
            def mm(dst, lhsT, rhs, start=True, stop=True, **kw):
                return pe.matmul(dst, lhsT, rhs, start=start, stop=stop, **kw)

            def tr(dst, src, n=128):
                return pe.transpose(dst, src, ident[0:n, 0:n])

            def small_transposes():
                pe.wait_ge(consts_set, 6)
                pe.wait_ge(attn_w_in, 64)
                pe.wait_ge(vec_in, 80)
                tr(bank[6][0:RANK, 0:128], lo_a[:, :])
                tr(bank[6][0:RANK, 128:256], lp_a[:, :])
                tr(bank[6][:, 256:256 + NV], vrow[:, :], NV).then_inc(small_tposed, 1)

            def lora_product():
                pe.wait_ge(lora_spread, 1)
                for n in range(3):
                    for j in range(3):
                        ins = mm(bank[7][:, n * C:(n + 1) * C], spread[:, j, n * 128:(n + 1) * 128],
                                 lo_b[:, j * C:(j + 1) * C], start=j == 0, stop=j == 2)
                ins.then_inc(lora_prod, 1)
                pe.wait_ge(proj_w_in, 32)
                mm(bank[3][:, 0:C], lp_b[:, :], lp_aT[:, :], stop=False)
                mm(bank[3][:, 0:C], wp[:, :], ident[:, :], start=False).then_inc(wmpT_done, 1)

            def wm_transposes():
                pe.wait_ge(wm_ready, 1)
                for n in range(3):
                    ins = tr(bank[7][:, n * C:(n + 1) * C], wm[:, n, :])
                ins.then_inc(wm_tposed, 1)
                pe.wait_ge(wmpT_copied, 1)
                mm(bank[3][:, C:2 * C], wp[:, :], wmpT[:, :]).then_inc(woT_done, 1)

            def spread_biases():
                pe.wait_ge(cross_w_in, 64)
                pe.wait_ge(wmT_copied, 1)
                mm(bank[7][:, 0:R_B1], ones[0:1, :], rrow[0:1, 0:R_B1]).then_inc(bias_spread, 1)

            def ctx_transpose(g):
                pe.wait_ge(c_in[g], 16)
                if g == 0:
                    pe.wait_ge(woT_copied, 1)
                if g >= 2:
                    pe.wait_ge(ct_copied, g - 1)
                for j in range(G):
                    ins = tr(bank[3 + g % 2][:, j * T:(j + 1) * T], cs[:, g * G + j, :])
                ins.then_inc(ct_done, 1)

            def ctx_k(g):
                pe.wait_ge(ct_copied, g + 1)
                for j in range(G):
                    b = g * G + j
                    ins = mm(bank[5][:, b * HD:(b + 1) * HD], cT[:, g % 2, j * T:(j + 1) * T], wqs[:, :])
                ins.then_inc(k_done, 1)

            small_transposes()
            lora_product()
            for g in range(NG):
                pe.wait_ge(normed, g + 1)
                if g >= 2:
                    pe.wait_ge(tcopied, g - 1)
                for j in range(G):
                    ins = tr(bank[1 + g % 2][:, j * T:(j + 1) * T], xn[:, g * G + j, 0:C])
                ins.then_inc(tposed, 1)
                for j in range(G):
                    b = g * G + j
                    ins = mm(bank[0][:, 0:C + 1], xn[:, b, 0:C], xn[:, b, :], start=b == 0, stop=b == B - 1)
                if g == 2:
                    wm_transposes()
                if g == 4:
                    spread_biases()
            ins.then_inc(gram_done, 1)
            ctx_transpose(0)
            ctx_transpose(1)
            ctx_k(0)
            pe.wait_ge(gram_copied, 1)
            for n in range(3):
                ins = mm(bank[6][:, n * (C + 1):(n + 1) * (C + 1)], wmT[:, n, :], gram[:, :])
            ins.then_inc(tg_done, 1)
            ctx_transpose(2)
            ctx_k(1)
            ctx_transpose(3)
            ctx_k(2)
            ctx_k(3)
            pe.wait_ge(dft_in, 48)
            pe.wait_ge(bias_copied, 1)
            mm(bank[7][:, 0:C], cosm[:, :], wouts[:, :])
            mm(bank[7][:, C:2 * C], sinm[:, :], wouts[:, :]).then_inc(wf_done, 1)
            pe.wait_ge(w3_ready, 1)
            mm(bank[6][:, 0:C], w3[:, 0, :], w3[:, 1, :])
            pe.wait_ge(woT_copied, 1)
            mm(bank[6][:, C:2 * C], w3[:, 2, :], woT[:, :]).then_inc(mqk_done, 1)
            for g in range(4, NG):
                ctx_transpose(g)
                ctx_k(g)

            def scores_left(g):
                if g == 0:
                    pe.wait_ge(mqk_copied, 1)
                    pe.wait_ge(tcopied, NG)
                else:
                    pe.wait_ge(g_copied, g)
                mm(bank[1][:, :], mqk[:, :], flat(grp(xnT, g))).then_inc(g_done, 1)

            def scores(g):
                pe.wait_ge(g_copied, g + 1)
                if g >= 2:
                    pe.wait_ge(exp_done, (g - 1) * G)
                mm(bank[2 + g % 2][:, :].rearrange("p (b t) -> p b t", b=G), identb[:, :],
                   maskb[:, :].unsqueeze(1).broadcast_to([T, G, T]), stop=False, skip_group_check=True)
                for j in range(G):
                    ins = mm(bank[2 + g % 2][:, j * T:(j + 1) * T], gT[:, g % 2, j * T:(j + 1) * T],
                             xnT[:, g * G + j, :], start=False, stop=j == G - 1, skip_group_check=True)
                ins.then_inc(s_done, 1)

            def p_transpose(g):
                pe.wait_ge(exp_done, (g + 1) * G)
                if g == 0:
                    pe.wait_ge(ct_copied, NG)
                else:
                    pe.wait_ge(pt_copied, g)
                for j in range(G):
                    ins = tr(bank[4][:, j * T:(j + 1) * T], p[:, g % 2, j, :])
                ins.then_inc(pt_done, 1)

            def weigh(g):
                pe.wait_ge(pt_copied, g + 1)
                if g:
                    pe.wait_ge(yt_copied, g)
                for j in range(G):
                    ins = mm(bank[6][:, j * T:(j + 1) * T], xn[:, g * G + j, 0:C], pT[:, g % 2, j * T:(j + 1) * T])
                ins.then_inc(yt_done, 1)

            def project(g):
                pe.wait_ge(yt_copied, g + 1)
                if g == 0:
                    pe.wait_ge(wf_copied, 1)
                else:
                    pe.wait_ge(resid, g)
                for j in range(G):
                    ins = mm(bank[7][:, j * C:(j + 1) * C], yT[:, g % 2, j * T:(j + 1) * T], wvo[:, :])
                ins.then_inc(y_done, 1)

            def ln_transpose(n, g):
                pe.wait_ge(normed, n * NG + g + 1)
                if n == 1 and g == 0:
                    pe.wait_ge(w1_ready, 1)
                else:
                    pe.wait_ge(tcopied, n * NG + g)
                for j in range(G):
                    ins = tr(bank[0][:, j * T:(j + 1) * T], ln[:, g % 2, j, :])
                ins.then_inc(tposed, 1)

            def cross_q(g):
                pe.wait_ge(tcopied, NG + g + 1)
                if g == 0:
                    pe.wait_ge(kv_ready, 1)
                for j in range(G):
                    b = g * G + j
                    ins = mm(bank[5][:, b * HD:(b + 1) * HD], lnT[:, g % 2, j * T:(j + 1) * T], wqs[:, :])
                ins.then_inc(q_done, 1)

            scores_left(0)
            for k in range(NG + 4):
                if k < NG:
                    scores(k)
                if 1 <= k <= NG:
                    p_transpose(k - 1)
                if k + 1 < NG:
                    scores_left(k + 1)
                if k == 0:
                    pe.wait_ge(kv_ready, 1)
                    mm(bank[0][:, 0:BH], cosm[:, :], kv[:, :])
                    mm(bank[0][:, BH:2 * BH], sinm[:, :], kv[:, :]).then_inc(kspec_done, 1)
                if k == 2:
                    pe.wait_ge(w1_in, 32)
                    pe.wait_ge(kspec_copied, 1)
                    mm(bank[0][:, :], negmean[:, :], w1s[:, :], stop=False)
                    mm(bank[0][:, :], inv128[0:1, :], rrow[0:1, R_B1:NR], start=False).then_inc(w1_mean, 1)
                if 1 <= k <= NG:
                    weigh(k - 1)
                if 3 <= k < NG + 3:
                    ln_transpose(1, k - 3)
                if 4 <= k:
                    cross_q(k - 4)
                if 1 <= k <= NG:
                    project(k - 1)

            pe.wait_ge(q_ready, 1)
            mm(bank[1][:, 0:BH], cosm[:, :], q[:, :])
            mm(bank[1][:, BH:2 * BH], sinm[:, :], q[:, :]).then_inc(qspec_done, 1)
            pe.wait_ge(power_ready, 1)
            mm(bank[2][:, 0:T], pwb[:, 0, :], cosm[:, :], stop=False)
            mm(bank[2][:, 0:T], pwb[:, 1, :], sinm[:, :], start=False).then_inc(corr_done, 1)
            pe.wait_ge(zspec_ready, 1)
            mm(bank[3][:, 0:C], cosm[:, :], ab[:, 2, :], stop=False)
            mm(bank[3][:, 0:C], sinm[:, :], ab[:, 3, :], start=False).then_inc(z_done, 1)

            def cross_out(g):
                pe.wait_ge(z_copied, 1)
                pe.wait_ge(v_repeated, g + 1)
                if g:
                    pe.wait_ge(resid, NG + g)
                for j in range(G):
                    ins = mm(bank[4][:, j * C:(j + 1) * C], cs[:, g * G + j, :], z[:, :])
                ins.then_inc(r_done, 1)

            def up(k):
                g, c = divmod(k, FC)
                pe.wait_ge(tcopied, 2 * NG + g + 1)
                if k >= 4:
                    pe.wait_ge(hid_done, k - 3)
                mm(bank[HB[k % 4]][:, :], w1p[:, c * 128:(c + 1) * 128], lnT[:, g % 2, :]).then_inc(h_done, 1)

            def down(k):
                g, c = divmod(k, FC)
                pe.wait_ge(relu_done, k + 1)
                if k == 0:
                    pe.wait_ge(w2_in, 16)
                if c == 0 and g >= 2:
                    pe.wait_ge(o_done, g - 1)
                for j in range(G):
                    ins = mm(bank[OB[g % 2]][:, j * C:(j + 1) * C], act_f[:, k % NACT, j * T:(j + 1) * T],
                             w2s[:, c, :], start=c == 0 and j == 0, stop=c == FC - 1 and j == G - 1,
                             skip_group_check=True)
                ins.then_inc(down_done, 1)

            cross_out(0)
            cross_out(1)
            ln_transpose(2, 0)
            for k in range(NCH + LAG):
                g, c = divmod(k, FC)
                if k < NCH:
                    up(k)
                if c == 0 and g + 2 < NG:
                    cross_out(g + 2)
                if c == 1 and g + 1 < NG:
                    ln_transpose(2, g + 1)
                if k >= LAG:
                    down(k - LAG)


_INS = ["x", "ctx_1024", "L0_attn_W_attn", "L0_attn_W_proj", "L0_attn_lora_attn_A", "L0_attn_lora_attn_B",
        "L0_attn_lora_proj_A", "L0_attn_lora_proj_B", "L0_attn_bn_gamma", "L0_attn_bn_beta", "L0_xattn_Wq",
        "L0_xattn_bq", "L0_xattn_Wout", "L0_xattn_bout", "L0_ffn_W1", "L0_ffn_b1", "L0_ffn_quantum_phases",
        "L0_ffn_quantum_weights_real", "L0_ffn_quantum_weights_imag", "L0_ffn_W2", "L0_ffn_b2"]


def kernel(**inputs):
    import concourse.bacc as bacc
    from concourse.bass_utils import run_bass_kernel_spmd

    nc = bacc.Bacc("TRN2", target_bir_lowering=False, num_devices=1)
    arrays, args = {}, []
    turns = np.outer(np.arange(T), np.arange(T)) % T * (TWO_PI / T)
    tables = {"dft_cos": np.cos(turns).astype(np.float32), "dft_sin": np.sin(turns).astype(np.float32)}
    for name in [*_INS, *tables]:
        a = np.ascontiguousarray(tables[name] if name in tables else inputs[name])
        arrays[f"in_{name}_dram"] = a
        args.append(nc.dram_tensor(f"in_{name}_dram", a.shape, mybir.dt.from_np(a.dtype), kind="ExternalInput").ap())
    args.append(nc.dram_tensor("out_0_dram", (B, T, C), FP32, kind="ExternalOutput").ap())
    decoder_layer(nc, *args)
    r = run_bass_kernel_spmd(nc, [arrays], core_ids=[0])
    return r.results[0]["out_0_dram"]
```

```python
import math
from contextlib import ExitStack

import numpy as np
import concourse.bass as bass
from concourse import mybir

FP32 = mybir.dt.float32
BF16 = mybir.dt.bfloat16
INT32 = mybir.dt.int32
ALU = mybir.AluOpType
ACT = mybir.ActivationFunctionType
AX = mybir.AxisListType

B, T, C = 32, 128, 128
G = 4
NG = B // G
W = G * T
RANK = 64
HD = 8
BH = B * HD
F = 512
FC = F // 128
EPS = 1e-5
K_TOP = int(2 * math.log(256))
TWO_PI = 2.0 * math.pi
PI_A = 6.28125
PI_B = float(np.float32(np.round((TWO_PI - PI_A) * 2**21) / 2**21))
PI_C = TWO_PI - PI_A - PI_B
ROUND = 1.5 * 2.0**23
INSIDE = 1.0 - 1e-6
FLT_MAX = 3.4028234663852886e38
MASKED = -1e30
PADDING, TAKEN = -2e38, -3e38
NV = 18
V_GAMMA, V_BETA, V_THETA, V_REAL, V_IMAG = 0, 3, 6, 10, 14
R_BOUT, R_B2, R_BQ, R_B1 = 0, C, 2 * C, 2 * C + HD
NR = R_B1 + F
LAG = 4
NCH = NG * FC
HB, OB = (1, 2, 3, 6), (5, 7)
SPANS = ((0, 1), (1, 1), (2, 2), (4, 2), (6, 1), (7, 1))
CG = 5
POOL_C = 2
NHID = 4
NACT = 6
(T_TURN, T_ANGLE, T_ROUND, T_RED, T_SIN, T_SINH, T_COS, T_MIX, T_KAPPA) = range(9)


def decoder_layer(nc, x, ctx_in, w_attn, w_proj, a_attn, b_attn, a_proj, b_proj, gamma, beta,
                  wq, bq, wout, bout, w1, b1, theta, w_real, w_imag, w2, b2, cos_t, sin_t, out):
    es = ExitStack()
    with es:
        def sb(name, shape, dt=FP32):
            return es.enter_context(nc.sbuf_tensor(name, shape, dt))

        def sem(name):
            return es.enter_context(nc.semaphore(name))

        xs = sb("xs", [T, B, C])
        cs = sb("cs", [T, B, C])
        xn = sb("xn", [T, B, C + 1])
        xnT = sb("xnT", [C, B, T])
        cT = sb("cT", [C, 2, W])
        ident = sb("ident", [128, 128])
        identb = sb("identb", [128, 128], BF16)
        maskb = sb("maskb", [T, T], BF16)
        cosm = sb("cosm", [T, T])
        sinm = sb("sinm", [T, T])
        ones = sb("ones", [128, 128])
        half = sb("half", [128, B])
        warm = sb("warm", [128, 1])
        vrow = sb("vrow", [NV, 128])
        vcol = sb("vcol", [128, NV])
        rrow = sb("rrow", [1, NR])
        inv128 = sb("inv128", [1, 128])
        negmean = sb("negmean", [128, 128])
        bc = sb("bc", [128, R_B1])
        wa = sb("wa", [128, 3, C])
        lo_a = sb("lo_a", [128, RANK])
        lo_b = sb("lo_b", [RANK, 3 * C])
        lp_a = sb("lp_a", [128, RANK])
        lp_b = sb("lp_b", [RANK, C])
        spread = sb("spread", [RANK, 3, 3 * C])
        lp_aT = sb("lp_aT", [RANK, 128])
        wp = sb("wp", [C, C])
        wmpT = sb("wmpT", [C, C])
        woT = sb("woT", [C, C])
        wm = sb("wm", [128, 3, C])
        wsum = sb("wsum", [128, 3])
        wmT = sb("wmT", [C, 3, C])
        gram = sb("gram", [C, C + 1])
        tg = sb("tg", [C, 3, C])
        q2 = sb("q2", [128, 3])
        mu = sb("mu", [128, 3])
        bn = sb("bn", [128, 8, 3])
        w3 = sb("w3", [128, 3, C])
        mqk = sb("mqk", [C, C])
        wvo = sb("wvo", [C, C])
        st = sb("st", [T, B, 6])
        mv = sb("mv", [T, B, 2])
        ve = sb("ve", [T, B])
        rstd = sb("rstd", [T, B])
        mr = sb("mr", [T, B])
        shift = sb("shift", [T, B])
        gT = sb("gT", [C, 2, W])
        p = sb("p", [T, 2, G, T])
        negmax = sb("negmax", [T, B])
        rowsum = sb("rowsum", [T, B])
        rinv = sb("rinv", [T, B])
        pT = sb("pT", [T, 2, W])
        yT = sb("yT", [C, 2, W])
        ln = sb("ln", [T, 2, G, C])
        lnT = sb("lnT", [C, 2, W])
        wqs = sb("wqs", [C, HD])
        wouts = sb("wouts", [T, C])
        kv = sb("kv", [T, BH])
        q = sb("q", [T, BH])
        kh = sb("kh", [T, 2, BH])
        kx = sb("kx", [T, 2, BH])
        junk = sb("junk", [128, 512])
        junk2 = sb("junk2", [128, 512])
        pw = sb("pw", [T, 2])
        pwb = sb("pwb", [T, 2, T])
        cw = sb("cw", [T, T + 8])
        cw2 = sb("cw2", [T, T + 8])
        cw3 = sb("cw3", [T, T + 8])
        top = sb("top", [T, 16])
        nmx = sb("nmx", [T, 1])
        ex = sb("ex", [T, T])
        sel = sb("sel", [T, T])
        ew = sb("ew", [T, T])
        wsm = sb("wsm", [T, 6])
        wf = sb("wf", [T, 2, C])
        ab = sb("ab", [T, 4, C])
        z = sb("z", [T, C])
        w1s = sb("w1s", [C, F])
        w1p = sb("w1p", [C, F])
        w2s = sb("w2s", [128, FC, C])
        th = sb("th", [128, 9, FC])
        turn = sb("turn", [128, 2, W], INT32)
        ang = sb("ang", [128, 2, W])
        sn = sb("sn", [128, 2, W])
        hid = sb("hid", [128, NHID, W])
        act_f = sb("act_f", [128, NACT, W])
        outs = sb("outs", [T, 2, G, C])

        bank = [es.enter_context(nc.psum_tensor(f"bank{i}", [128, 512], FP32)) for i in range(8)]

        x_in = [sem(f"x_in{g}") for g in range(NG)]
        c_in = [sem(f"c_in{g}") for g in range(NG)]
        attn_w_in, vec_in, proj_w_in, cross_w_in, rows_in, dft_in, w1_in, w2_in = (
            sem(n) for n in ("attn_w_in", "vec_in", "proj_w_in", "cross_w_in", "rows_in", "dft_in", "w1_in", "w2_in"))
        out_sent = [sem("out_sent0"), sem("out_sent1")]
        (consts_set, small_tposed, vec_tposed, lora_spread, vec_copied, lora_prod, wm_ready, wm_tposed, wmT_copied,
         wmpT_done, wmpT_copied, woT_done, woT_copied, bias_spread, bias_copied, gram_done, gram_copied,
         tg_done, bn_var, bn_rstd, bn_ready, w3_ready, w3v_ready, wvo_copied, mqk_done, mqk_copied, wf_done, wf_copied, kv_ready, kspec_done,
         kspec_copied, w1_mean, w1_ready, theta_ready, sines_done, q_ready, qspec_done,
         power_ready, corr_done, corr_copied, top_ready, lag_exp, zspec_ready, z_done, z_copied) = (
            sem(n) for n in (
                "consts_set", "small_tposed", "vec_tposed", "lora_spread", "vec_copied", "lora_prod", "wm_ready", "wm_tposed",
                "wmT_copied", "wmpT_done", "wmpT_copied", "woT_done", "woT_copied", "bias_spread", "bias_copied",
                "gram_done", "gram_copied", "tg_done", "bn_var", "bn_rstd", "bn_ready", "w3_ready", "w3v_ready", "wvo_copied", "mqk_done", "mqk_copied",
                "wf_done", "wf_copied", "kv_ready", "kspec_done", "kspec_copied", "w1_mean", "w1_ready",
                "theta_ready", "sines_done", "q_ready", "qspec_done", "power_ready", "corr_done",
                "corr_copied", "top_ready", "lag_exp", "zspec_ready", "z_done", "z_copied"))
        pool_seq = sem("pool_seq")
        dve_seq = sem("dve_seq")
        stats = sem("stats")
        scaled = sem("scaled")
        normed = sem("normed")
        normed_a = sem("normed_a")
        tposed = sem("tposed")
        tcopied = sem("tcopied")
        resid = sem("resid")
        biased = sem("biased")
        (ct_done, ct_copied, k_done, g_done, g_copied, s_done, max_done, pt_done, pt_copied, yt_done, yt_copied,
         y_done, q_done, r_done, o_done) = (
            sem(n) for n in ("ct_done", "ct_copied", "k_done", "g_done", "g_copied", "s_done", "max_done",
                             "pt_done", "pt_copied", "yt_done", "yt_copied", "y_done", "q_done", "r_done", "o_done"))
        v_repeated = sem("v_repeated")
        exp_done = sem("exp_done")
        h_done, turn_done, ang_done, sin_done, hid_done, down_done = (
            sem(n) for n in ("h_done", "turn_done", "ang_done", "sin_done", "hid_done", "down_done"))
        relu_a_done, relu_p_done = sem("relu_a_done"), sem("relu_p_done")

        block = es.enter_context(nc.Block())

        def grp(t, g):
            return t[:, g * G:(g + 1) * G, :]

        def flat(ap):
            return ap.rearrange("p a b -> p (a b)")

        def wait_relu(eng, k):
            if k % FC == POOL_C:
                eng.wait_ge(relu_p_done, k // FC + 1)
            else:
                eng.wait_ge(relu_a_done, k // FC * (FC - 1) + k % FC + (k % FC < POOL_C))

        @block.sync
        def _(sp):
            for g in range(NG):
                sp.dma_start(grp(xs, g), x[g * G:(g + 1) * G].rearrange("b t c -> t b c")).then_inc(x_in[g], 16)
            sp.dma_start(wp[:, :], w_proj).then_inc(proj_w_in, 16)
            sp.dma_start(lp_b[:, :], b_proj).then_inc(proj_w_in, 16)
            sp.dma_start(wqs[:, :], wq).then_inc(cross_w_in, 16)
            for at, n, src in ((R_BOUT, C, bout), (R_B2, C, b2), (R_BQ, HD, bq)):
                sp.dma_start(rrow[0:1, at:at + n], src.unsqueeze(0)).then_inc(rows_in, 16)
            for at, n, src in ((V_GAMMA, 3, gamma), (V_BETA, 3, beta), (V_THETA, FC, theta),
                               (V_REAL, FC, w_real), (V_IMAG, FC, w_imag)):
                sp.dma_start(vrow[at:at + n, :], src.rearrange("(n p) -> n p", p=128)).then_inc(vec_in, 16)
            for g in range(NG):
                sp.dma_start(grp(cs, g), ctx_in[g * G:(g + 1) * G].rearrange("b t c -> t b c")).then_inc(c_in[g], 16)
            for dst, src in ((cosm, cos_t), (sinm, sin_t), (wouts, wout)):
                sp.dma_start(dst[:, :], src).then_inc(dft_in, 16)
            sp.dma_start(w1s[:, :], w1).then_inc(w1_in, 16)
            sp.dma_start(rrow[0:1, R_B1:NR], b1.unsqueeze(0)).then_inc(w1_in, 16)
            sp.dma_start(w2s[:, :, :], w2.rearrange("(f p) d -> p f d", p=128)).then_inc(w2_in, 16)
            for g in range(NG):
                sp.wait_ge(o_done, g + 1)
                sp.dma_start(out[g * G:(g + 1) * G].rearrange("b t c -> t b c"),
                             outs[:, g % 2, :, :]).then_inc(out_sent[g % 2], 16)
            sp.wait_ge(out_sent[0], 16 * (NG // 2))
            sp.wait_ge(out_sent[1], 16 * (NG // 2))

        @block.gpsimd
        def _(pool):
            seq = [0]

            def after(ins):
                seq[0] += 1
                ins.then_inc(pool_seq, 1)
                pool.wait_ge(pool_seq, seq[0])

            pool.memset(ident[:, :], 0.0).then_inc(pool_seq, 1)
            pool.memset(maskb[:, :], 0.0).then_inc(pool_seq, 1)
            seq[0] += 2
            pool.wait_ge(pool_seq, seq[0])
            after(pool.affine_select(out=ident[:, :], in_=ident[:, :], compare_op=ALU.not_equal, fill=1.0,
                                     base=0, pattern=[[-1, 128]], channel_multiplier=1))
            pool.affine_select(out=maskb[:, :], in_=maskb[:, :], compare_op=ALU.is_ge, fill=MASKED,
                               base=0, pattern=[[-1, 128]], channel_multiplier=1).then_inc(consts_set, 1)
            pool.tensor_copy(identb[:, :], ident[:, :]).then_inc(consts_set, 1)
            after(pool.memset(half[:, :], -0.5))
            pool.memset(ones[:, :], 1.0).then_inc(consts_set, 1)
            pool.memset(inv128[:, :], 1.0 / 128).then_inc(consts_set, 1)
            pool.memset(negmean[:, :], -1.0 / 128).then_inc(consts_set, 1)
            pool.memset(xn[:, :, C:C + 1], 1.0).then_inc(consts_set, 1)

            def scale_group(n, g, add, groups=1):
                a, b = g * G, (g + groups) * G
                pool.wait_ge(stats, n * NG + g + groups)
                after(pool.tensor_scalar(ve[:, a:b], mv[:, a:b, 1], EPS, 1.0, ALU.add, ALU.mult))
                after(pool.tensor_tensor(rstd[:, a:b], ve[:, a:b], half[:, a:b], ALU.pow))
                after(pool.tensor_tensor(mr[:, a:b], mv[:, a:b, 0], rstd[:, a:b], ALU.mult))
                return pool.tensor_scalar(shift[:, a:b], mr[:, a:b], -1.0, add, ALU.mult, ALU.add)

            def norm_group(n, g, add):
                after(scale_group(n, g, add))
                if g >= 2 or n == 2:
                    pool.wait_ge(tposed, n * NG + g - 1)
                for j in range(G):
                    b = g * G + j
                    ins = pool.tensor_scalar(ln[:, g % 2, j, :], xs[:, b, :], rstd[:, b:b + 1], shift[:, b:b + 1],
                                             ALU.mult, ALU.add)
                ins.then_inc(normed, 1)

            def add_bias(n, g, at):
                pool.wait_ge(normed, n * NG + g + 1)
                row = bc[:, at:at + C].unsqueeze(1).broadcast_to([128, G, C])
                pool.tensor_tensor(grp(xs, g), grp(xs, g), row, ALU.add).then_inc(biased, 1)

            for g, groups in SPANS:
                scale_group(0, g, 1.0, groups).then_inc(scaled, groups)
            pool.wait_ge(bn_var, 1)
            pool.tensor_tensor(bn[:, 1, :], bn[:, 0, :], half[:, 0:3], ALU.pow).then_inc(bn_rstd, 1)
            pool.wait_ge(bias_copied, 1)
            for g in range(NG):
                norm_group(1, g, 0.0)
            for g in range(NG):
                add_bias(1, g, R_BOUT)

            def relu(k):
                pool.wait_ge(hid_done, k + 1)
                if k >= NACT:
                    pool.wait_ge(down_done, k - NACT + 1)
                pool.tensor_scalar(act_f[:, k % NACT, :], hid[:, k % NHID, :], FLT_MAX, 0.0, ALU.min,
                                   ALU.max).then_inc(relu_p_done, 1)

            for g in (0, 1):
                norm_group(2, g, 1.0)
                add_bias(2, g, R_B2)
            for k in range(NCH):
                g, c = divmod(k, FC)
                if c == POOL_C:
                    relu(k)
                if c == 1 and g + 2 < NG:
                    norm_group(2, g + 2, 1.0)
                if c == 2 and g + 2 < NG:
                    add_bias(2, g + 2, R_B2)

        @block.scalar
        def _(act):
            def load(sem_, dst, src):
                act.dma_start(dst, src).then_inc(sem_, 16)

            load(attn_w_in, lo_a[:, :], a_attn)
            load(attn_w_in, lp_a[:, :], a_proj)
            load(attn_w_in, lo_b[:, :], b_attn)
            load(attn_w_in, wa[:, :, :], w_attn.rearrange("(n p) c -> p n c", p=128))

            def copy(dst, src, scale=1.0):
                return act.activation(dst, src, ACT.Copy, scale=scale)

            def copy_xT(g):
                act.wait_ge(tposed, g + 1)
                copy(flat(grp(xnT, g)), bank[1 + g % 2][:, :]).then_inc(tcopied, 1)

            def copy_cT(g):
                act.wait_ge(ct_done, g + 1)
                if g >= 2:
                    act.wait_ge(k_done, g - 1)
                copy(cT[:, g % 2, :], bank[3 + g % 2][:, :]).then_inc(ct_copied, 1)

            def norm0(g):
                act.wait_ge(scaled, g + 1)
                for j in range(G // 2):
                    b = g * G + j
                    ins = act.activation(xn[:, b, 0:C], xs[:, b, :], ACT.Identity, scale=rstd[:, b:b + 1],
                                         bias=shift[:, b:b + 1])
                ins.then_inc(normed_a, 1)

            act.wait_ge(consts_set, 6)
            act.activation(warm[:, :], half[:, 0:1], ACT.Exp)
            norm0(0)
            for g in range(NG):
                if g + 1 < NG:
                    norm0(g + 1)
                copy_xT(g)
                if g == 1:
                    act.wait_ge(wmpT_done, 1)
                    copy(wmpT[:, :], bank[3][:, 0:C]).then_inc(wmpT_copied, 1)
                if g == 3:
                    act.wait_ge(wm_tposed, 1)
                    copy(flat(wmT[:, :, :]), bank[7][:, 0:3 * C]).then_inc(wmT_copied, 1)
                    act.wait_ge(woT_done, 1)
                    copy(woT[:, :], bank[3][:, C:2 * C]).then_inc(woT_copied, 1)
                if g == 4:
                    act.wait_ge(bias_spread, 1)
                    copy(bc[:, :], bank[7][:, 0:R_B1]).then_inc(bias_copied, 1)
                if g >= CG:
                    copy_cT(g - CG)
            act.wait_ge(gram_done, 1)
            copy(gram[:, :], bank[0][:, 0:C + 1], scale=1.0 / (B * T)).then_inc(gram_copied, 1)
            for g in range(NG - CG, NG - 1):
                copy_cT(g)
            act.wait_ge(bn_ready, 1)
            act.activation(w3[:, 2, :], wm[:, 2, :], ACT.Identity, scale=bn[:, 3, 2:3],
                           bias=bn[:, 4, 2:3]).then_inc(w3v_ready, 1)
            act.wait_ge(mqk_done, 1)
            copy(mqk[:, :], bank[6][:, 0:C], scale=float(C) ** -0.5).then_inc(mqk_copied, 1)
            copy(wvo[:, :], bank[6][:, C:2 * C]).then_inc(wvo_copied, 1)
            act.wait_ge(wf_done, 1)
            copy(flat(wf[:, :, :]), bank[7][:, 0:2 * C]).then_inc(wf_copied, 1)
            def copy_g(g):
                act.wait_ge(g_done, g + 1)
                if g >= 2:
                    act.wait_ge(s_done, g - 1)
                copy(gT[:, g % 2, :], bank[1][:, :]).then_inc(g_copied, 1)

            def copy_pT(g):
                act.wait_ge(pt_done, g + 1)
                if g >= 2:
                    act.wait_ge(yt_done, g - 1)
                copy(pT[:, g % 2, :], bank[4][:, :]).then_inc(pt_copied, 1)

            def exps(g, js):
                act.wait_ge(max_done, g + 1)
                if g >= 2:
                    act.wait_ge(pt_done, g - 1)
                for j in js:
                    b = g * G + j
                    act.activation(p[:, g % 2, j, :], bank[2 + g % 2][:, j * T:(j + 1) * T], ACT.Exp,
                                   bias=negmax[:, b:b + 1], accum_out=rowsum[:, b:b + 1]).then_inc(exp_done, 1)

            def copy_lnT(n, g):
                act.wait_ge(tposed, n * NG + g + 1)
                if n == 1 and g >= 2:
                    act.wait_ge(q_done, g - 1)
                if n == 2:
                    act.wait_ge(q_done, NG) if g < 2 else act.wait_ge(h_done, (g - 1) * FC)
                copy(lnT[:, g % 2, :], bank[0][:, :]).then_inc(tcopied, 1)

            copy_g(0)
            copy_cT(NG - 1)
            for k in range(NG + 3):
                if 1 <= k <= NG:
                    copy_pT(k - 1)
                if k < NG:
                    exps(k, (0, 1))
                if k + 1 < NG:
                    copy_g(k + 1)
                if k < NG:
                    exps(k, (2, 3))
                if 3 <= k:
                    copy_lnT(1, k - 3)

            act.wait_ge(top_ready, 1)
            act.activation(ex[:, :], cw[:, 0:T], ACT.Exp, bias=nmx[:, 0:1]).then_inc(lag_exp, 1)
            act.wait_ge(theta_ready, 1)
            act.activation(th[:, T_SIN, :], th[:, T_ANGLE, :], ACT.Sin)
            act.activation(th[:, T_SINH, :], th[:, T_ANGLE, :], ACT.Sin, scale=0.5).then_inc(sines_done, 1)
            act.wait_ge(z_done, 1)
            copy(z[:, :], bank[3][:, 0:C]).then_inc(z_copied, 1)

            def turns(k):
                act.wait_ge(h_done, k + 1)
                if k >= 2:
                    act.wait_ge(ang_done, k - 1)
                act.activation(turn[:, k % 2, :], bank[HB[k % 4]][:, :], ACT.Identity, scale=0.1 / TWO_PI,
                               bias=th[:, T_TURN, k % FC:k % FC + 1]).then_inc(turn_done, 1)

            def sine(k):
                act.wait_ge(ang_done, k + 1)
                if k >= 2:
                    act.wait_ge(hid_done, k - 1)
                act.activation(sn[:, k % 2, :], ang[:, k % 2, :], ACT.Sin, scale=TWO_PI * INSIDE,
                               bias=th[:, T_ANGLE, k % FC:k % FC + 1]).then_inc(sin_done, 1)

            def relu(k):
                act.wait_ge(hid_done, k + 1)
                if k >= NACT:
                    act.wait_ge(down_done, k - NACT + 1)
                act.activation(act_f[:, k % NACT, :], hid[:, k % NHID, :], ACT.Relu).then_inc(relu_a_done, 1)

            copy_lnT(2, 0)
            for k in range(NCH + 2):
                if k < NCH:
                    turns(k)
                if 1 <= k <= NCH:
                    sine(k - 1)
                if k >= 2 and (k - 2) % FC != POOL_C:
                    relu(k - 2)
                if k % FC == 2 and k // FC + 1 < NG:
                    copy_lnT(2, k // FC + 1)

        @block.vector
        def _(dve):
            seq = [0]

            def after(ins):
                seq[0] += 1
                ins.then_inc(dve_seq, 1)
                dve.wait_ge(dve_seq, seq[0])

            def copy(dst, src):
                return dve.tensor_copy(dst, src)

            def group_stats(g):
                for j in range(G):
                    ins = dve.bn_stats(st[:, g * G + j, :], xs[:, g * G + j, :])
                after(ins)
                for j in range(G):
                    ins = dve.bn_aggr(mv[:, g * G + j, :], st[:, g * G + j, :])
                ins.then_inc(stats, 1)

            def norm0(g):
                dve.wait_ge(scaled, g + 1)
                for j in range(G // 2, G):
                    b = g * G + j
                    ins = dve.tensor_scalar(xn[:, b, 0:C], xs[:, b, :], rstd[:, b:b + 1], shift[:, b:b + 1],
                                            ALU.mult, ALU.add)
                ins.then_inc(normed, 1)

            def spread_lora():
                dve.wait_ge(small_tposed, 1)
                for j in range(3):
                    copy(spread[:, j, :].rearrange("r (i k) -> r i k", k=3)[:, :, j], bank[6][0:RANK, 0:128])
                copy(lp_aT[:, :], bank[6][0:RANK, 128:256]).then_inc(lora_spread, 1)

            def copy_vectors():
                dve.wait_ge(vec_tposed, 1)
                copy(vcol[:, :], bank[6][:, 256:256 + NV]).then_inc(vec_copied, 1)

            def centre_weights():
                dve.wait_ge(lora_prod, 1)
                after(dve.tensor_tensor(flat(wm[:, :, :]), bank[7][:, 0:3 * C], flat(wa[:, :, :]), ALU.add))
                after(dve.reduce_sum(wsum[:, :], wm[:, :, :], AX.X))
                after(dve.tensor_scalar(wsum[:, :], wsum[:, :], 1.0 / C, None, ALU.mult))
                for n in range(3):
                    ins = dve.tensor_scalar(wm[:, n, :], wm[:, n, :], wsum[:, n:n + 1], None, ALU.subtract)
                ins.then_inc(wm_ready, 1)

            def col(i):
                return th[:, i, :]

            def reduce_theta():
                theta_c = vcol[:, V_THETA:V_THETA + FC]
                dve.wait_ge(vec_copied, 1)
                after(dve.tensor_scalar(col(T_ROUND), theta_c, 1.0 / TWO_PI, ROUND, ALU.mult, ALU.add))
                after(dve.tensor_scalar(col(T_ROUND), col(T_ROUND), ROUND, None, ALU.subtract))
                after(dve.scalar_tensor_tensor(col(T_RED), col(T_ROUND), -PI_A, theta_c, ALU.mult, ALU.add))
                after(dve.scalar_tensor_tensor(col(T_RED), col(T_ROUND), -PI_B, col(T_RED), ALU.mult, ALU.add))
                after(dve.scalar_tensor_tensor(col(T_RED), col(T_ROUND), -PI_C, col(T_RED), ALU.mult, ALU.add))
                dve.tensor_scalar(col(T_TURN), col(T_RED), 1.0 / TWO_PI, None, ALU.mult)
                dve.tensor_scalar(col(T_ANGLE), col(T_RED), INSIDE, None, ALU.mult).then_inc(theta_ready, 1)

            def make_kappa():
                wr, wi = vcol[:, V_REAL:V_REAL + FC], vcol[:, V_IMAG:V_IMAG + FC]
                dve.wait_ge(sines_done, 1)
                after(dve.tensor_tensor(col(T_COS), col(T_SINH), col(T_SINH), ALU.mult))
                after(dve.tensor_scalar(col(T_COS), col(T_COS), -2.0, 1.0, ALU.mult, ALU.add))
                after(dve.tensor_tensor(col(T_COS), col(T_COS), wr, ALU.mult))
                after(dve.tensor_tensor(col(T_MIX), col(T_SIN), wi, ALU.mult))
                after(dve.tensor_tensor(col(T_MIX), col(T_MIX), col(T_COS), ALU.add))
                after(dve.tensor_tensor(col(T_MIX), col(T_MIX), wi, ALU.mult))
                after(dve.tensor_scalar(col(T_KAPPA), col(T_MIX), 0.1, None, ALU.mult))

            dve.memset(spread[:, :, :], 0.0)
            for g in range(NG):
                dve.wait_ge(x_in[g], 16)
                group_stats(g)
                if g >= 2:
                    norm0(g - 2)
                if g == 2:
                    spread_lora()
                if g == 4:
                    centre_weights()
                if g == 7:
                    copy_vectors()
            norm0(NG - 2)
            norm0(NG - 1)

            dve.wait_ge(tg_done, 1)
            copy(mu[:, :], bank[6][:, 0:3 * (C + 1)].rearrange("p (n c) -> p n c", n=3)[:, :, C])
            for n in range(3):
                ins = dve.tensor_tensor_reduce(out=tg[:, n, :], in0=bank[6][:, n * (C + 1):n * (C + 1) + C],
                                               in1=wm[:, n, :], scale=1.0, scalar=0.0, op0=ALU.mult, op1=ALU.add,
                                               accum_out=q2[:, n:n + 1])
            after(ins)
            after(dve.tensor_tensor(bn[:, 2, :], mu[:, :], mu[:, :], ALU.mult))
            dve.scalar_tensor_tensor(bn[:, 0, :], q2[:, :], EPS, bn[:, 2, :], ALU.add,
                                     ALU.subtract).then_inc(bn_var, 1)
            dve.tensor_scalar(bn[:, 6, :], vcol[:, V_BETA:V_BETA + 3], 1.0 / C, None, ALU.mult)
            after(dve.scalar_tensor_tensor(bn[:, 5, :], mu[:, :], -1.0 / C, vcol[:, V_GAMMA:V_GAMMA + 3],
                                           ALU.mult, ALU.mult))
            dve.wait_ge(bn_rstd, 1)
            dve.tensor_tensor(bn[:, 3, :], bn[:, 1, :], vcol[:, V_GAMMA:V_GAMMA + 3], ALU.mult)
            after(dve.tensor_tensor(bn[:, 7, :], bn[:, 1, :], bn[:, 5, :], ALU.mult))
            dve.tensor_tensor(bn[:, 4, :], bn[:, 7, :], bn[:, 6, :], ALU.add).then_inc(bn_ready, 1)
            dve.wait_ge(bn_ready, 1)
            for n in range(2):
                ins = dve.tensor_scalar(w3[:, n, :], wm[:, n, :], bn[:, 3, n:n + 1], bn[:, 4, n:n + 1],
                                        ALU.mult, ALU.add)
            ins.then_inc(w3_ready, 1)
            reduce_theta()

            bqb = bc[:, R_BQ:R_BQ + HD].unsqueeze(1).broadcast_to([128, B, HD])

            def heads(ap):
                return ap.rearrange("p (b h) -> p b h", h=HD)

            def row_max(g):
                dve.wait_ge(s_done, g + 1)
                dve.tensor_reduce(negmax[:, g * G:(g + 1) * G],
                                  bank[2 + g % 2][:, :].rearrange("p (b t) -> p b t", b=G),
                                  AX.X, ALU.max, negate=True).then_inc(max_done, 1)

            def add_y(g):
                dve.wait_ge(exp_done, (g + 1) * G)
                after(dve.reciprocal(rinv[:, g * G:(g + 1) * G], rowsum[:, g * G:(g + 1) * G]))
                dve.wait_ge(y_done, g + 1)
                for j in range(G):
                    b = g * G + j
                    ins = dve.scalar_tensor_tensor(xs[:, b, :], bank[7][:, j * C:(j + 1) * C], rinv[:, b:b + 1],
                                                   xs[:, b, :], ALU.mult, ALU.add)
                ins.then_inc(resid, 1)

            def copy_yT(g):
                dve.wait_ge(yt_done, g + 1)
                if g >= 2:
                    dve.wait_ge(y_done, g - 1)
                copy(yT[:, g % 2, :], bank[6][:, :]).then_inc(yt_copied, 1)

            def repeat_v(g):
                dve.tensor_copy(grp(cs, g).rearrange("p b (r h) -> p b r h", h=HD),
                                kv[:, g * G * HD:(g + 1) * G * HD].rearrange("p (b h) -> p b h", h=HD)
                                .unsqueeze(2).broadcast_to([T, G, T // HD, HD])).then_inc(v_repeated, 1)

            for k in range(NG + 2):
                if 2 <= k:
                    add_y(k - 2)
                if k < NG:
                    row_max(k)
                if k == 0:
                    dve.wait_ge(k_done, NG)
                    dve.wait_ge(bias_copied, 1)
                    dve.tensor_tensor(heads(kv[:, :]), heads(bank[5][:, 0:BH]), bqb, ALU.add).then_inc(kv_ready, 1)
                    dve.wait_ge(kv_ready, 1)
                if k < NG:
                    repeat_v(k)
                if 2 <= k:
                    dve.wait_ge(resid, k - 1)
                    group_stats(k - 2)
                if 1 <= k <= NG:
                    copy_yT(k - 1)
                if k == 1:
                    dve.wait_ge(kspec_done, 1)
                    copy(flat(kh[:, :, :]), bank[0][:, :])
                    copy(kx[:, 0, :], bank[0][:, BH:2 * BH])
                    dve.tensor_scalar(kx[:, 1, :], bank[0][:, 0:BH], -1.0, None, ALU.mult).then_inc(kspec_copied, 1)
                if k == 2:
                    dve.wait_ge(w1_mean, 1)
                    dve.tensor_tensor(w1p[:, :], bank[0][:, :], w1s[:, :], ALU.add).then_inc(w1_ready, 1)

            dve.wait_ge(q_done, NG)
            dve.tensor_tensor(heads(q[:, :]), heads(bank[5][:, 0:BH]), bqb, ALU.add).then_inc(q_ready, 1)
            dve.wait_ge(qspec_done, 1)
            dve.tensor_tensor_reduce(out=junk[:, :], in0=bank[1][:, :], in1=flat(kh[:, :, :]), scale=1.0, scalar=0.0,
                                     op0=ALU.mult, op1=ALU.add, accum_out=pw[:, 0:1])
            after(dve.tensor_tensor_reduce(out=junk2[:, :], in0=bank[1][:, :], in1=flat(kx[:, :, :]), scale=1.0,
                                           scalar=0.0, op0=ALU.mult, op1=ALU.add, accum_out=pw[:, 1:2]))
            dve.tensor_scalar(pwb[:, 0, :], ones[:, :], pw[:, 0:1], 1.0 / (T * BH), ALU.mult, ALU.mult)
            dve.tensor_scalar(pwb[:, 1, :], ones[:, :], pw[:, 1:2], -1.0 / (T * BH), ALU.mult,
                              ALU.mult).then_inc(power_ready, 1)
            dve.memset(cw[:, T:T + 8], PADDING)
            dve.wait_ge(corr_done, 1)
            copy(cw[:, 0:T], bank[2][:, 0:T]).then_inc(corr_copied, 1)
            dve.wait_ge(corr_copied, 1)
            after(dve.max(top[:, 0:8], cw[:, :]))
            dve.tensor_scalar(nmx[:, :], top[:, 0:1], -1.0, None, ALU.mult).then_inc(top_ready, 1)
            after(dve.match_replace(cw2[:, :], top[:, 0:8], cw[:, :], TAKEN))
            after(dve.max(top[:, 8:16], cw2[:, :]))
            after(dve.memset(top[:, K_TOP:16], PADDING))
            after(dve.match_replace(cw3[:, :], top[:, 8:16], cw2[:, :], TAKEN))
            after(dve.tensor_scalar(sel[:, :], cw3[:, 0:T], TAKEN, None, ALU.is_equal))
            dve.wait_ge(lag_exp, 1)
            after(dve.tensor_tensor_reduce(out=ew[:, :], in0=ex[:, :], in1=sel[:, :], scale=1.0, scalar=0.0,
                                           op0=ALU.mult, op1=ALU.add, accum_out=wsm[:, 0:1]))
            dve.tensor_tensor_reduce(out=junk[:, 0:T], in0=ew[:, :], in1=cosm[:, :], scale=1.0, scalar=0.0,
                                     op0=ALU.mult, op1=ALU.add, accum_out=wsm[:, 1:2])
            dve.tensor_tensor_reduce(out=junk2[:, 0:T], in0=ew[:, :], in1=sinm[:, :], scale=1.0, scalar=0.0,
                                     op0=ALU.mult, op1=ALU.add, accum_out=wsm[:, 2:3])
            after(dve.reciprocal(wsm[:, 3:4], wsm[:, 0:1]))
            after(dve.tensor_scalar(wsm[:, 4:6], wsm[:, 1:3], wsm[:, 3:4], 1.0 / T, ALU.mult, ALU.mult))
            dve.wait_ge(wf_copied, 1)
            dve.tensor_scalar(ab[:, 0, :], wf[:, 1, :], wsm[:, 5:6], None, ALU.mult)
            after(dve.tensor_scalar(ab[:, 1, :], wf[:, 0, :], wsm[:, 5:6], None, ALU.mult))
            dve.scalar_tensor_tensor(ab[:, 2, :], wf[:, 0, :], wsm[:, 4:5], ab[:, 0, :], ALU.mult, ALU.subtract)
            dve.scalar_tensor_tensor(ab[:, 3, :], wf[:, 1, :], wsm[:, 4:5], ab[:, 1, :], ALU.mult,
                                     ALU.add).then_inc(zspec_ready, 1)

            def add_cross(g):
                dve.wait_ge(r_done, g + 1)
                dve.wait_ge(biased, g + 1)
                dve.tensor_tensor(flat(grp(xs, g)), bank[4][:, :], flat(grp(xs, g)), ALU.add).then_inc(resid, 1)
                dve.wait_ge(resid, NG + g + 1)
                group_stats(g)

            def angle(k):
                dve.wait_ge(turn_done, k + 1)
                if k >= 2:
                    dve.wait_ge(sin_done, k - 1)
                dve.scalar_tensor_tensor(ang[:, k % 2, :], bank[HB[k % 4]][:, :], 0.1 / TWO_PI, turn[:, k % 2, :],
                                         ALU.mult, ALU.subtract).then_inc(ang_done, 1)

            def hidden(k):
                dve.wait_ge(sin_done, k + 1)
                if k >= NHID:
                    wait_relu(dve, k - NHID)
                c = k % FC
                dve.scalar_tensor_tensor(hid[:, k % NHID, :], sn[:, k % 2, :], th[:, T_KAPPA, c:c + 1],
                                         bank[HB[k % 4]][:, :], ALU.mult, ALU.add).then_inc(hid_done, 1)

            def output(g):
                dve.wait_ge(down_done, (g + 1) * FC)
                dve.wait_ge(biased, NG + g + 1)
                if g >= 2:
                    dve.wait_ge(out_sent[g % 2], 16 * (g // 2))
                dve.tensor_tensor(flat(outs[:, g % 2, :, :]), bank[OB[g % 2]][:, :], flat(grp(xs, g)),
                                  ALU.add).then_inc(o_done, 1)

            make_kappa()
            add_cross(0)
            add_cross(1)
            for k in range(NCH + LAG + 2):
                if k < NCH:
                    angle(k)
                if 1 <= k <= NCH:
                    hidden(k - 1)
                if k % FC == 0 and k // FC + 2 < NG:
                    add_cross(k // FC + 2)
                if k >= LAG + FC and (k - LAG) % FC == 1:
                    output((k - LAG) // FC - 1)

        @block.tensor
        def _(pe):
            def mm(dst, lhsT, rhs, start=True, stop=True, **kw):
                return pe.matmul(dst, lhsT, rhs, start=start, stop=stop, **kw)

            def tr(dst, src, n=128):
                return pe.transpose(dst, src, ident[0:n, 0:n])

            def small_transposes():
                pe.wait_ge(attn_w_in, 64)
                tr(bank[6][0:RANK, 0:128], lo_a[:, :])
                tr(bank[6][0:RANK, 128:256], lp_a[:, :]).then_inc(small_tposed, 1)

            def vec_transposes():
                pe.wait_ge(vec_in, 80)
                pe.wait_ge(lora_spread, 1)
                tr(bank[6][:, 256:256 + NV], vrow[:, :], NV).then_inc(vec_tposed, 1)

            def lora_product():
                pe.wait_ge(lora_spread, 1)
                for n in range(3):
                    for j in range(3):
                        ins = mm(bank[7][:, n * C:(n + 1) * C], spread[:, j, n * 128:(n + 1) * 128],
                                 lo_b[:, j * C:(j + 1) * C], start=j == 0, stop=j == 2)
                ins.then_inc(lora_prod, 1)
                pe.wait_ge(proj_w_in, 32)
                mm(bank[3][:, 0:C], lp_b[:, :], lp_aT[:, :], stop=False)
                mm(bank[3][:, 0:C], wp[:, :], ident[:, :], start=False).then_inc(wmpT_done, 1)

            def wm_transposes():
                pe.wait_ge(wm_ready, 1)
                for n in range(3):
                    ins = tr(bank[7][:, n * C:(n + 1) * C], wm[:, n, :])
                ins.then_inc(wm_tposed, 1)
                pe.wait_ge(wmpT_copied, 1)
                mm(bank[3][:, C:2 * C], wp[:, :], wmpT[:, :]).then_inc(woT_done, 1)

            def spread_biases():
                pe.wait_ge(rows_in, 48)
                pe.wait_ge(wmT_copied, 1)
                mm(bank[7][:, 0:R_B1], ones[0:1, :], rrow[0:1, 0:R_B1]).then_inc(bias_spread, 1)

            def ctx_transpose(g):
                pe.wait_ge(c_in[g], 16)
                if g == 0:
                    pe.wait_ge(woT_copied, 1)
                if g >= 2:
                    pe.wait_ge(ct_copied, g - 1)
                for j in range(G):
                    ins = tr(bank[3 + g % 2][:, j * T:(j + 1) * T], cs[:, g * G + j, :])
                ins.then_inc(ct_done, 1)

            def ctx_k(g):
                if g == 0:
                    pe.wait_ge(cross_w_in, 16)
                pe.wait_ge(ct_copied, g + 1)
                for j in range(G):
                    b = g * G + j
                    ins = mm(bank[5][:, b * HD:(b + 1) * HD], cT[:, g % 2, j * T:(j + 1) * T], wqs[:, :])
                ins.then_inc(k_done, 1)

            pe.wait_ge(consts_set, 6)
            for g in range(NG):
                pe.wait_ge(normed, g + 1)
                pe.wait_ge(normed_a, g + 1)
                if g >= 2:
                    pe.wait_ge(tcopied, g - 1)
                for j in range(G):
                    ins = tr(bank[1 + g % 2][:, j * T:(j + 1) * T], xn[:, g * G + j, 0:C])
                ins.then_inc(tposed, 1)
                for j in range(G):
                    b = g * G + j
                    ins = mm(bank[0][:, 0:C + 1], xn[:, b, 0:C], xn[:, b, :], start=b == 0, stop=b == B - 1)
                if g == NG - 1:
                    ins.then_inc(gram_done, 1)
                if g == 0:
                    small_transposes()
                if g == 0:
                    lora_product()
                if g == 3:
                    wm_transposes()
                if g == 4:
                    spread_biases()
                    vec_transposes()
                if g >= CG:
                    ctx_transpose(g - CG)
                if g > CG:
                    ctx_k(g - CG - 1)
            ctx_transpose(NG - CG)
            pe.wait_ge(gram_copied, 1)
            pe.wait_ge(vec_copied, 1)
            for n in range(3):
                ins = mm(bank[6][:, n * (C + 1):(n + 1) * (C + 1)], wmT[:, n, :], gram[:, :])
            ins.then_inc(tg_done, 1)
            ctx_k(NG - CG - 1)
            for g in range(NG - CG + 1, NG - 1):
                ctx_transpose(g)
                ctx_k(g - 1)
            pe.wait_ge(dft_in, 48)
            pe.wait_ge(bias_copied, 1)
            mm(bank[7][:, 0:C], cosm[:, :], wouts[:, :])
            mm(bank[7][:, C:2 * C], sinm[:, :], wouts[:, :]).then_inc(wf_done, 1)
            pe.wait_ge(w3_ready, 1)
            mm(bank[6][:, 0:C], w3[:, 0, :], w3[:, 1, :])
            pe.wait_ge(w3v_ready, 1)
            mm(bank[6][:, C:2 * C], w3[:, 2, :], woT[:, :]).then_inc(mqk_done, 1)
            def scores_left(g):
                if g == 0:
                    pe.wait_ge(mqk_copied, 1)
                    pe.wait_ge(tcopied, NG)
                else:
                    pe.wait_ge(g_copied, g)
                mm(bank[1][:, :], mqk[:, :], flat(grp(xnT, g))).then_inc(g_done, 1)

            def scores(g):
                pe.wait_ge(g_copied, g + 1)
                if g >= 2:
                    pe.wait_ge(exp_done, (g - 1) * G)
                mm(bank[2 + g % 2][:, :].rearrange("p (b t) -> p b t", b=G), identb[:, :],
                   maskb[:, :].unsqueeze(1).broadcast_to([T, G, T]), stop=False, skip_group_check=True)
                for j in range(G):
                    ins = mm(bank[2 + g % 2][:, j * T:(j + 1) * T], gT[:, g % 2, j * T:(j + 1) * T],
                             xnT[:, g * G + j, :], start=False, stop=j == G - 1, skip_group_check=True)
                ins.then_inc(s_done, 1)

            def p_transpose(g):
                pe.wait_ge(exp_done, (g + 1) * G)
                if g == 0:
                    pe.wait_ge(ct_copied, NG)
                else:
                    pe.wait_ge(pt_copied, g)
                for j in range(G):
                    ins = tr(bank[4][:, j * T:(j + 1) * T], p[:, g % 2, j, :])
                ins.then_inc(pt_done, 1)

            def weigh(g):
                pe.wait_ge(pt_copied, g + 1)
                if g == 0:
                    pe.wait_ge(wvo_copied, 1)
                else:
                    pe.wait_ge(yt_copied, g)
                for j in range(G):
                    ins = mm(bank[6][:, j * T:(j + 1) * T], xn[:, g * G + j, 0:C], pT[:, g % 2, j * T:(j + 1) * T])
                ins.then_inc(yt_done, 1)

            def project(g):
                pe.wait_ge(yt_copied, g + 1)
                if g == 0:
                    pe.wait_ge(wf_copied, 1)
                else:
                    pe.wait_ge(resid, g)
                for j in range(G):
                    ins = mm(bank[7][:, j * C:(j + 1) * C], yT[:, g % 2, j * T:(j + 1) * T], wvo[:, :])
                ins.then_inc(y_done, 1)

            def ln_transpose(n, g):
                pe.wait_ge(normed, n * NG + g + 1)
                if n == 1 and g == 0:
                    pe.wait_ge(w1_ready, 1)
                else:
                    pe.wait_ge(tcopied, n * NG + g)
                for j in range(G):
                    ins = tr(bank[0][:, j * T:(j + 1) * T], ln[:, g % 2, j, :])
                ins.then_inc(tposed, 1)

            def cross_q(g):
                pe.wait_ge(tcopied, NG + g + 1)
                if g == 0:
                    pe.wait_ge(kv_ready, 1)
                for j in range(G):
                    b = g * G + j
                    ins = mm(bank[5][:, b * HD:(b + 1) * HD], lnT[:, g % 2, j * T:(j + 1) * T], wqs[:, :])
                ins.then_inc(q_done, 1)

            scores_left(0)
            ctx_transpose(NG - 1)
            ctx_k(NG - 2)
            for k in range(NG + 4):
                if k < NG:
                    scores(k)
                if k == 0:
                    ctx_k(NG - 1)
                if 1 <= k <= NG:
                    p_transpose(k - 1)
                if k + 1 < NG:
                    scores_left(k + 1)
                if k == 1:
                    pe.wait_ge(kv_ready, 1)
                    mm(bank[0][:, 0:BH], cosm[:, :], kv[:, :])
                    mm(bank[0][:, BH:2 * BH], sinm[:, :], kv[:, :]).then_inc(kspec_done, 1)
                if k == 2:
                    pe.wait_ge(w1_in, 32)
                    pe.wait_ge(kspec_copied, 1)
                    mm(bank[0][:, :], negmean[:, :], w1s[:, :], stop=False)
                    mm(bank[0][:, :], inv128[0:1, :], rrow[0:1, R_B1:NR], start=False).then_inc(w1_mean, 1)
                if 1 <= k <= NG:
                    weigh(k - 1)
                if 3 <= k < NG + 3:
                    ln_transpose(1, k - 3)
                if 4 <= k:
                    cross_q(k - 4)
                if 1 <= k <= NG:
                    project(k - 1)

            pe.wait_ge(q_ready, 1)
            mm(bank[1][:, 0:BH], cosm[:, :], q[:, :])
            mm(bank[1][:, BH:2 * BH], sinm[:, :], q[:, :]).then_inc(qspec_done, 1)
            pe.wait_ge(power_ready, 1)
            mm(bank[2][:, 0:T], pwb[:, 0, :], cosm[:, :], stop=False)
            mm(bank[2][:, 0:T], pwb[:, 1, :], sinm[:, :], start=False).then_inc(corr_done, 1)
            pe.wait_ge(zspec_ready, 1)
            mm(bank[3][:, 0:C], cosm[:, :], ab[:, 2, :], stop=False)
            mm(bank[3][:, 0:C], sinm[:, :], ab[:, 3, :], start=False).then_inc(z_done, 1)

            def cross_out(g):
                pe.wait_ge(z_copied, 1)
                pe.wait_ge(v_repeated, g + 1)
                if g:
                    pe.wait_ge(resid, NG + g)
                for j in range(G):
                    ins = mm(bank[4][:, j * C:(j + 1) * C], cs[:, g * G + j, :], z[:, :])
                ins.then_inc(r_done, 1)

            def up(k):
                g, c = divmod(k, FC)
                pe.wait_ge(tcopied, 2 * NG + g + 1)
                if k >= 4:
                    pe.wait_ge(hid_done, k - 3)
                mm(bank[HB[k % 4]][:, :], w1p[:, c * 128:(c + 1) * 128], lnT[:, g % 2, :]).then_inc(h_done, 1)

            def down(k):
                g, c = divmod(k, FC)
                wait_relu(pe, k)
                if k == 0:
                    pe.wait_ge(w2_in, 16)
                if c == 0 and g >= 2:
                    pe.wait_ge(o_done, g - 1)
                for j in range(G):
                    ins = mm(bank[OB[g % 2]][:, j * C:(j + 1) * C], act_f[:, k % NACT, j * T:(j + 1) * T],
                             w2s[:, c, :], start=c == 0 and j == 0, stop=c == FC - 1 and j == G - 1,
                             skip_group_check=True)
                ins.then_inc(down_done, 1)

            cross_out(0)
            cross_out(1)
            ln_transpose(2, 0)
            for k in range(NCH + LAG):
                g, c = divmod(k, FC)
                if k < NCH:
                    up(k)
                if c == 0 and g + 2 < NG:
                    cross_out(g + 2)
                if c == 1 and g + 1 < NG:
                    ln_transpose(2, g + 1)
                if k >= LAG:
                    down(k - LAG)


_INS = ["x", "ctx_1024", "L0_attn_W_attn", "L0_attn_W_proj", "L0_attn_lora_attn_A", "L0_attn_lora_attn_B",
        "L0_attn_lora_proj_A", "L0_attn_lora_proj_B", "L0_attn_bn_gamma", "L0_attn_bn_beta", "L0_xattn_Wq",
        "L0_xattn_bq", "L0_xattn_Wout", "L0_xattn_bout", "L0_ffn_W1", "L0_ffn_b1", "L0_ffn_quantum_phases",
        "L0_ffn_quantum_weights_real", "L0_ffn_quantum_weights_imag", "L0_ffn_W2", "L0_ffn_b2"]


def kernel(**inputs):
    import concourse.bacc as bacc
    from concourse.bass_utils import run_bass_kernel_spmd

    nc = bacc.Bacc("TRN2", target_bir_lowering=False, num_devices=1)
    arrays, args = {}, []
    turns = np.outer(np.arange(T), np.arange(T)) % T * (TWO_PI / T)
    tables = {"dft_cos": np.cos(turns).astype(np.float32), "dft_sin": np.sin(turns).astype(np.float32)}
    for name in [*_INS, *tables]:
        a = np.ascontiguousarray(tables[name] if name in tables else inputs[name])
        arrays[f"in_{name}_dram"] = a
        args.append(nc.dram_tensor(f"in_{name}_dram", a.shape, mybir.dt.from_np(a.dtype), kind="ExternalInput").ap())
    args.append(nc.dram_tensor("out_0_dram", (B, T, C), FP32, kind="ExternalOutput").ap())
    decoder_layer(nc, *args)
    r = run_bass_kernel_spmd(nc, [arrays], core_ids=[0])
    return r.results[0]["out_0_dram"]
```

```python
import math
from contextlib import ExitStack

import numpy as np
import concourse.bass as bass
from concourse import mybir

FP32 = mybir.dt.float32
BF16 = mybir.dt.bfloat16
INT32 = mybir.dt.int32
ALU = mybir.AluOpType
ACT = mybir.ActivationFunctionType
AX = mybir.AxisListType

B, T, C = 32, 128, 128
G = 4
NG = B // G
W = G * T
RANK = 64
HD = 8
BH = B * HD
F = 512
FC = F // 128
EPS = 1e-5
K_TOP = int(2 * math.log(256))
TWO_PI = 2.0 * math.pi
PI_A = 6.28125
PI_B = float(np.float32(np.round((TWO_PI - PI_A) * 2**21) / 2**21))
PI_C = TWO_PI - PI_A - PI_B
ROUND = 1.5 * 2.0**23
INSIDE = 1.0 - 1e-6
MASKED = -1e30
PADDING, TAKEN = -2e38, -3e38
V_GAMMA, V_BETA, V_THETA, V_REAL, V_IMAG, V_B1, NV = 0, 3, 6, 10, 14, 18, 22
R_BOUT, R_B2, R_BQ, NR = 0, C, 2 * C, 2 * C + HD
WARM_UP = 14
LAG = 5
NCH = NG * FC
HB, OB, RB, AHEAD = (1, 2, 3, 6), (5, 7), (4, 5, 7, 4), 3
YB = (7, 0)
FIRST_DVE = 3
KPART = (0, 5, NG)
TB = (3, 4, 3, 4, 3, 1, 2, 3)
QPART, SB = (0, NG - 2, NG), (3, 1)
POOL_C = 2
NHID = 4
NACT = 7
P_IN, P_ROUND, P_RED, P_TURN, P_ANGLE = range(5)
B_VAR, B_RSTD, B_MEAN2, B_SCALE, B_SHIFT, B_GMEAN, B_BETA, B_GMEAN_STD = range(8)
L_SUM, L_COS, L_SIN, L_INV, L_SCALE = range(5)
A_SS, A_CS, A_COS, A_SIN = range(4)
T_SIN, T_SINH, T_COS, T_MIX, T_KAPPA = range(5)


def decoder_layer(nc, x, ctx_in, w_attn, w_proj, a_attn, b_attn, a_proj, b_proj, gamma, beta,
                  wq, bq, wout, bout, w1, b1, theta, w_real, w_imag, w2, b2, cos_t, sin_t, out):
    es = ExitStack()
    with es:
        def sb(name, shape, dt=FP32):
            return es.enter_context(nc.sbuf_tensor(name, shape, dt))

        def sem(name):
            return es.enter_context(nc.semaphore(name))

        xs = sb("xs", [T, B, C])
        cs = sb("cs", [T, B, C])
        xn = sb("xn", [T, B, C + 1])
        xnT = sb("xnT", [C, B, T])
        cT = sb("cT", [C, 2, W])
        ident = sb("ident", [128, 128])
        identb = sb("identb", [128, 128], BF16)
        maskb = sb("maskb", [T, T], BF16)
        cosm = sb("cosm", [T, T])
        sinm = sb("sinm", [T, T])
        ones = sb("ones", [128, 128])
        half = sb("half", [128, B])
        warm = sb("warm", [128, 1])
        zeros = sb("zeros", [128, 512], BF16)
        vrow = sb("vrow", [NV, 128])
        vcol = sb("vcol", [128, NV])
        rrow = sb("rrow", [1, NR])
        negmean = sb("negmean", [128, 128])
        bc = sb("bc", [128, NR + HD])
        wa = sb("wa", [128, 3, C])
        lo_a = sb("lo_a", [128, RANK])
        lo_b = sb("lo_b", [RANK, 3 * C])
        lp_a = sb("lp_a", [128, RANK])
        lp_b = sb("lp_b", [RANK, C])
        lo_aT = sb("lo_aT", [RANK, 128])
        lp_aT = sb("lp_aT", [RANK, 128])
        wp = sb("wp", [C, C])
        wmpT = sb("wmpT", [C, C])
        wox = sb("wox", [C, 2, C + HD])
        wm3 = sb("wm3", [128, 3, C])
        wm = sb("wm", [128, 3, C])
        wsum = sb("wsum", [128, 3])
        wmT = sb("wmT", [C, 3, C])
        gram = sb("gram", [C, C + 1])
        tg = sb("tg", [C, 3, C])
        q2 = sb("q2", [128, 3])
        mu = sb("mu", [128, 3])
        bn = sb("bn", [128, 8, 3])
        w3 = sb("w3", [128, 3, C])
        mqk = sb("mqk", [C, C])
        wvo = sb("wvo", [C, C + HD])
        st = sb("st", [T, B, 6])
        mv = sb("mv", [T, B, 2])
        ve = sb("ve", [T, B])
        rstd = sb("rstd", [T, B])
        mr = sb("mr", [T, B])
        shift = sb("shift", [T, B])
        gT = sb("gT", [C, 2, W])
        p = sb("p", [T, 2, G, T])
        negmax = sb("negmax", [T, B])
        rowsum = sb("rowsum", [T, B])
        rinv = sb("rinv", [T, B])
        pT = sb("pT", [T, 2, W])
        yT = sb("yT", [C, 2, W])
        ln = sb("ln", [T, 2, G, C])
        lnT = sb("lnT", [C, 2, W])
        wqs = sb("wqs", [C, HD])
        wqc = sb("wqc", [C, HD])
        wouts = sb("wouts", [T, C])
        kv = sb("kv", [T, BH])
        q = sb("q", [T, BH])
        std0 = sb("std0", [T, B])
        qx = sb("qx", [T, BH])
        qy = sb("qy", [T, BH])
        kh = sb("kh", [T, 2, BH])
        kx = sb("kx", [T, 2, BH])
        junk = sb("junk", [128, 512])
        junk2 = sb("junk2", [128, 512])
        pw = sb("pw", [T, 4])
        cw = sb("cw", [T, T + 8])
        cw2 = sb("cw2", [T, T + 8])
        top = sb("top", [T, 16])
        nmx = sb("nmx", [T, 1])
        ex = sb("ex", [T, T])
        ew = sb("ew", [T, T])
        wsm = sb("wsm", [T, 5])
        negb1 = sb("negb1", [128, 1])
        b1rep = sb("b1rep", [128, 128])
        wf = sb("wf", [T, 2, C])
        ab = sb("ab", [T, 4, C])
        z = sb("z", [T, C])
        w1s = sb("w1s", [C, F])
        w2s = sb("w2s", [128, FC, C])
        ph = sb("ph", [128, 5, 2, FC])
        th = sb("th", [128, 5, FC])
        turn = sb("turn", [128, 2, W], INT32)
        ang = sb("ang", [128, 2, W])
        sn = sb("sn", [128, 2, W])
        hid = sb("hid", [128, NHID, W])
        act_f = sb("act_f", [128, NACT, W])
        outs = sb("outs", [T, 2, G, C])

        bank = [es.enter_context(nc.psum_tensor(f"bank{i}", [128, 512], FP32)) for i in range(8)]

        x_in = [sem(f"x_in{g}") for g in range(NG)]
        c_in = [sem(f"c_in{g}") for g in range(NG)]
        attn_w_in, vec_in, proj_w_in, cross_w_in, rows_in, dft_in, w1_in, w2_in = (
            sem(n) for n in "attn_w_in vec_in proj_w_in cross_w_in rows_in dft_in w1_in w2_in".split())
        out_sent = [sem("out_sent0"), sem("out_sent1")]
        (zeros_set, consts_set, small_tposed, vec_tposed, lora_copied, vec_copied, lora_prod, lora_added,
         wm3_ready, wm3_tposed, wmT_copied, wm_tposed, wm_copied, wmpT_done, wmpT_copied, woT_done,
         woT_copied, wqc_ready, woq_done, woq_copied, bias_spread, bias_copied) = (
            sem(n) for n in (
                "zeros_set consts_set small_tposed vec_tposed lora_copied vec_copied lora_prod lora_added "
                "wm3_ready wm3_tposed wmT_copied wm_tposed wm_copied wmpT_done wmpT_copied woT_done "
                "woT_copied wqc_ready woq_done woq_copied bias_spread bias_copied").split())
        (gram_done, gram_copied, tg_done, bn_var, bn_rstd, bn_ready, w3_ready, w3v_ready, mqk_done,
         mqk_copied, wvo_copied) = (
            sem(n) for n in (
                "gram_done gram_copied tg_done bn_var bn_rstd bn_ready w3_ready w3v_ready mqk_done mqk_copied "
                "wvo_copied").split())
        (wf_done, wf_copied, kv_ready, kspec_done, kspec_copied, q_taken, q_ready, qspec_done, power_ready,
         corr_done, top_ready, lag_exp, weights_ready, lag_scaled, zspec_ready, lag_sum, z_done, z_copied) = (
            sem(n) for n in (
                "wf_done wf_copied kv_ready kspec_done kspec_copied q_taken q_ready qspec_done power_ready "
                "corr_done top_ready lag_exp weights_ready lag_scaled zspec_ready lag_sum z_done z_copied").split())
        b1_repeated, b1w2_done, b2_ready, theta_ready, sines_done = (
            sem(n) for n in "b1_repeated b1w2_done b2_ready theta_ready sines_done".split())
        pool_seq = sem("pool_seq")
        dve_seq = sem("dve_seq")
        stats = sem("stats")
        scaled = sem("scaled")
        normed = sem("normed")
        tposed = sem("tposed")
        tcopied = sem("tcopied")
        normed_a = sem("normed_a")
        first_normed = sem("first_normed")
        resid = sem("resid")
        biased = sem("biased")
        ct_done, ct_copied, k_done = sem("ct_done"), sem("ct_copied"), sem("k_done")
        g_done, g_copied = sem("g_done"), sem("g_copied")
        s_done, max_done = sem("s_done"), sem("max_done")
        pt_done, pt_copied = sem("pt_done"), sem("pt_copied")
        yt_done, yt_copied = sem("yt_done"), sem("yt_copied")
        y_done, q_done = sem("y_done"), sem("q_done")
        r_done, o_done = sem("r_done"), sem("o_done")
        v_repeated, v_repeated_p = sem("v_repeated"), sem("v_repeated_p")
        exp_done = sem("exp_done")
        h_done, turn_done, ang_done, sin_done, hid_done, down_done = (
            sem(n) for n in ("h_done", "turn_done", "ang_done", "sin_done", "hid_done", "down_done"))
        relu_a_done, relu_p_done = sem("relu_a_done"), sem("relu_p_done")

        block = es.enter_context(nc.Block())

        def grp(t, g):
            return t[:, g * G:(g + 1) * G, :]

        def flat(ap):
            return ap.rearrange("p a b -> p (a b)")

        def y_part(j):
            return bank[YB[j // 2]][:, j % 2 * (C + HD):(j % 2 + 1) * (C + HD)]

        def repeat_v(eng, g):
            return eng.tensor_copy(grp(cs, g).rearrange("p b (r h) -> p b r h", h=HD),
                                   kv[:, g * G * HD:(g + 1) * G * HD].rearrange("p (b h) -> p b h", h=HD)
                                   .unsqueeze(2).broadcast_to([T, G, T // HD, HD]))

        def b1_col(k):
            return vcol[:, V_B1 + k % FC:V_B1 + k % FC + 1]

        def wait_relu(eng, k):
            if k % FC == POOL_C:
                eng.wait_ge(relu_p_done, k // FC + 1)
            else:
                eng.wait_ge(relu_a_done, k // FC * (FC - 1) + k % FC + (k % FC < POOL_C))

        @block.sync
        def _(sp):
            for g in range(NG):
                sp.dma_start(grp(xs, g), x[g * G:(g + 1) * G].rearrange("b t c -> t b c")).then_inc(x_in[g], 16)
            sp.dma_start(wp[:, :], w_proj).then_inc(proj_w_in, 16)
            sp.dma_start(lp_b[:, :], b_proj).then_inc(proj_w_in, 16)
            sp.dma_start(wqs[:, :], wq).then_inc(cross_w_in, 16)
            for at, n, src in ((R_BOUT, C, bout), (R_B2, C, b2), (R_BQ, HD, bq)):
                sp.dma_start(rrow[0:1, at:at + n], src.unsqueeze(0)).then_inc(rows_in, 16)
            for at, n, src in ((V_GAMMA, 3, gamma), (V_BETA, 3, beta), (V_THETA, FC, theta),
                               (V_REAL, FC, w_real), (V_IMAG, FC, w_imag), (V_B1, FC, b1)):
                sp.dma_start(vrow[at:at + n, :], src.rearrange("(n p) -> n p", p=128)).then_inc(vec_in, 16)
            for g in range(NG):
                sp.dma_start(grp(cs, g),
                             ctx_in[g * G:(g + 1) * G].rearrange("b t c -> t b c")).then_inc(c_in[g], 16)
            for dst, src in ((cosm, cos_t), (sinm, sin_t), (wouts, wout)):
                sp.dma_start(dst[:, :], src).then_inc(dft_in, 16)
            sp.dma_start(w1s[:, :], w1).then_inc(w1_in, 16)
            sp.dma_start(w2s[:, :, :], w2.rearrange("(f p) d -> p f d", p=128)).then_inc(w2_in, 16)
            for g in range(NG - 1):
                sp.wait_ge(o_done, g + 1)
                sp.dma_start(out[g * G:(g + 1) * G].rearrange("b t c -> t b c"),
                             outs[:, g % 2, :, :]).then_inc(out_sent[g % 2], 16)
            for part, (a, b) in enumerate(((0, G // 2), (G // 2, G))):
                sp.wait_ge(o_done, NG + part)
                sp.dma_start(out[(NG - 1) * G + a:(NG - 1) * G + b].rearrange("b t c -> t b c"),
                             outs[:, (NG - 1) % 2, a:b, :]).then_inc(out_sent[(NG - 1) % 2], 16)
            sp.wait_ge(out_sent[0], 16 * (NG // 2))
            sp.wait_ge(out_sent[1], 16 * (NG // 2 + 1))

        @block.gpsimd
        def _(pool):
            seq = [0]

            def after(ins):
                seq[0] += 1
                ins.then_inc(pool_seq, 1)
                pool.wait_ge(pool_seq, seq[0])

            pool.memset(ident[:, :], 0.0).then_inc(pool_seq, 1)
            pool.memset(maskb[:, :], 0.0).then_inc(pool_seq, 1)
            seq[0] += 2
            pool.wait_ge(pool_seq, seq[0])
            after(pool.affine_select(out=ident[:, :], in_=ident[:, :], compare_op=ALU.not_equal, fill=1.0,
                                     base=0, pattern=[[-1, 128]], channel_multiplier=1))
            pool.affine_select(out=maskb[:, :], in_=maskb[:, :], compare_op=ALU.is_ge, fill=MASKED,
                               base=0, pattern=[[-1, 128]], channel_multiplier=1).then_inc(consts_set, 1)
            pool.tensor_copy(identb[:, :], ident[:, :]).then_inc(consts_set, 1)
            after(pool.memset(half[:, :], -0.5))
            pool.memset(ones[:, :], 1.0).then_inc(consts_set, 1)
            pool.memset(negmean[:, :], -1.0 / 128).then_inc(consts_set, 1)
            pool.memset(xn[:, :, C:C + 1], 1.0).then_inc(consts_set, 1)

            def std_group(n, g):
                a, b = g * G, (g + 1) * G
                pool.wait_ge(stats, n * NG + g + 1)
                after(pool.tensor_scalar(ve[:, a:b], mv[:, a:b, 1], EPS, None, ALU.add))
                return pool.tensor_tensor(rstd[:, a:b], ve[:, a:b], half[:, a:b], ALU.pow)

            def scale_group(n, g, add):
                a, b = g * G, (g + 1) * G
                after(std_group(n, g))
                after(pool.tensor_tensor(mr[:, a:b], mv[:, a:b, 0], rstd[:, a:b], ALU.mult))
                return pool.tensor_scalar(shift[:, a:b], mr[:, a:b], -1.0, add, ALU.mult, ALU.add)

            def norm_group(g):
                if g == 0:
                    std_group(2, g).then_inc(scaled, 1)
                    pool.wait_ge(scaled, 2 * NG + 1)
                    for b in range(FIRST_DVE, G):
                        ins = pool.tensor_scalar(ln[:, 0, b, :], xs[:, b, :], mv[:, b, 0:1], rstd[:, b:b + 1],
                                                 ALU.subtract, ALU.mult)
                    ins.then_inc(normed, 1)
                    return
                after(scale_group(2, g, 0.0))
                if g >= 2:
                    pool.wait_ge(tposed, NG + g - 1)
                for j in range(G):
                    b = g * G + j
                    ins = pool.tensor_scalar(ln[:, g % 2, j, :], xs[:, b, :], rstd[:, b:b + 1], shift[:, b:b + 1],
                                             ALU.mult, ALU.add)
                ins.then_inc(normed, 1)

            def add_bias(n, g, at):
                if n == 1:
                    pool.wait_ge(stats, NG + g + 1)
                else:
                    pool.wait_ge(normed, NG + g + 1)
                    if g == 0:
                        pool.wait_ge(first_normed, FIRST_DVE)
                        pool.wait_ge(b2_ready, 1)
                row = bc[:, at:at + C].unsqueeze(1).broadcast_to([128, G, C])
                pool.tensor_tensor(grp(xs, g), grp(xs, g), row, ALU.add).then_inc(biased, 1)

            for g in range(NG):
                scale_group(0, g, 1.0).then_inc(scaled, 1)
            pool.wait_ge(bn_var, 1)
            pool.tensor_tensor(bn[:, B_RSTD, :], bn[:, B_VAR, :], half[:, 0:3], ALU.pow).then_inc(bn_rstd, 1)
            pool.wait_ge(bias_copied, 1)
            for g in range(NG):
                std_group(1, g).then_inc(scaled, 1)
                add_bias(1, g, R_BOUT)

            pool.wait_ge(kv_ready, 2)
            for g in range(KPART[1], NG):
                repeat_v(pool, g).then_inc(v_repeated_p, 1)

            def relu(k):
                pool.wait_ge(hid_done, k + 1)
                if k >= NACT:
                    pool.wait_ge(down_done, k - NACT + 1)
                pool.tensor_scalar(act_f[:, k % NACT, :], hid[:, k % NHID, :], negb1[:, :], None,
                                   ALU.max).then_inc(relu_p_done, 1)

            for g in (0, 1):
                norm_group(g)
            for g in (0, 1):
                add_bias(2, g, R_B2)
            for k in range(NCH):
                g, c = divmod(k, FC)
                if c == POOL_C:
                    relu(k)
                if c == 1 and g + 2 < NG:
                    norm_group(g + 2)
                if c == 2 and g + 2 < NG:
                    add_bias(2, g + 2, R_B2)

        @block.scalar
        def _(act):
            def load(sem_, dst, src):
                act.dma_start(dst, src).then_inc(sem_, 16)

            load(attn_w_in, lo_a[:, :], a_attn)
            load(attn_w_in, lp_a[:, :], a_proj)
            load(attn_w_in, lo_b[:, :], b_attn)
            load(attn_w_in, wa[:, :, :], w_attn.rearrange("(p n) c -> p n c", n=3))

            def copy(dst, src, scale=1.0):
                return act.activation(dst, src, ACT.Copy, scale=scale)

            def copy_xT(g):
                act.wait_ge(tposed, g + 1)
                copy(flat(grp(xnT, g)), bank[1 + g % 2][:, :]).then_inc(tcopied, 1)

            def copy_cT(g):
                act.wait_ge(ct_done, g + 1)
                if g >= 2:
                    act.wait_ge(k_done, g - 1)
                copy(cT[:, g % 2, :], bank[TB[g]][:, :]).then_inc(ct_copied, 1)

            def norm0(g):
                act.wait_ge(scaled, g + 1)
                for j in range(G // 2):
                    b = g * G + j
                    ins = act.activation(xn[:, b, 0:C], xs[:, b, :], ACT.Identity, scale=rstd[:, b:b + 1],
                                         bias=shift[:, b:b + 1])
                ins.then_inc(normed_a, 1)

            act.wait_ge(consts_set, 5)
            act.activation(warm[:, :], half[:, 0:1], ACT.Exp)
            norm0(0)
            for g in range(NG):
                if g + 1 < NG:
                    norm0(g + 1)
                copy_xT(g)
                if g == 1:
                    act.wait_ge(lora_added, 1)
                    for n in range(3):
                        ins = act.activation(wm3[:, n, :], wa[:, n, :], ACT.Identity, bias=wsum[:, n:n + 1])
                    ins.then_inc(wm3_ready, 1)
                    act.wait_ge(wmpT_done, 1)
                    copy(wmpT[:, :], bank[3][:, 0:C]).then_inc(wmpT_copied, 1)
                if g == 3:
                    act.wait_ge(woT_done, 1)
                    copy(wox[:, :, 0:C],
                         bank[3][:, C:3 * C].rearrange("p (n c) -> p n c", n=2)).then_inc(woT_copied, 1)
                    act.wait_ge(wm3_tposed, 1)
                    copy(flat(wmT[:, :, :]).rearrange("p (i n) -> p n i", n=3),
                         bank[7][:, 0:3 * C].rearrange("p (n i) -> p n i", n=3)).then_inc(wmT_copied, 1)
                if g == 4:
                    act.wait_ge(wm_tposed, 1)
                    copy(flat(wm[:, :, :]), bank[7][:, 0:3 * C]).then_inc(wm_copied, 1)
                if g == 5:
                    act.wait_ge(bias_spread, 1)
                    copy(bc[:, :], bank[7][:, 0:NR + HD]).then_inc(bias_copied, 1)
            copy_cT(0)
            act.wait_ge(gram_done, 1)
            copy(gram[:, :], bank[0][:, 0:C + 1], scale=1.0 / (B * T)).then_inc(gram_copied, 1)
            copy_cT(1)
            act.wait_ge(woq_done, 1)
            copy(wox[:, 0, C:C + HD], bank[0][:, 0:HD]).then_inc(woq_copied, 1)
            copy_cT(2)
            copy_cT(3)
            act.wait_ge(bn_ready, 1)
            act.activation(w3[:, 2, :], wm[:, 2, :], ACT.Identity, scale=bn[:, B_SCALE, 2:3],
                           bias=bn[:, B_SHIFT, 2:3]).then_inc(w3v_ready, 1)
            act.wait_ge(mqk_done, 1)
            copy(mqk[:, :], bank[6][:, 0:C], scale=float(C) ** -0.5).then_inc(mqk_copied, 1)
            copy(wvo[:, :], bank[6][:, C:2 * C + HD]).then_inc(wvo_copied, 1)
            act.wait_ge(wf_done, 1)
            copy(flat(wf[:, :, :]), bank[7][:, 0:2 * C]).then_inc(wf_copied, 1)
            copy_cT(NG - 4)
            def copy_g(g):
                act.wait_ge(g_done, g + 1)
                if g >= 2:
                    act.wait_ge(s_done, g - 1)
                copy(gT[:, g % 2, :], bank[1][:, :]).then_inc(g_copied, 1)

            def copy_pT(g):
                act.wait_ge(pt_done, g + 1)
                if g >= 2:
                    act.wait_ge(yt_done, g - 1)
                copy(pT[:, g % 2, :], bank[4][:, :]).then_inc(pt_copied, 1)

            def exps(g, js):
                act.wait_ge(max_done, g + 1)
                if g >= 2:
                    act.wait_ge(pt_done, g - 1)
                for j in js:
                    b = g * G + j
                    act.activation(p[:, g % 2, j, :], bank[2 + g % 2][:, j * T:(j + 1) * T], ACT.Exp,
                                   bias=negmax[:, b:b + 1], accum_out=rowsum[:, b:b + 1]).then_inc(exp_done, 1)

            def copy_yT(g):
                act.wait_ge(yt_done, g + 1)
                if g >= 2:
                    act.wait_ge(y_done, g - 1)
                copy(yT[:, g % 2, :], bank[6][:, :]).then_inc(yt_copied, 1)

            def copy_lnT(g):
                act.wait_ge(tposed, NG + g + 1)
                if g >= 2:
                    act.wait_ge(h_done, (g - 1) * FC)
                copy(lnT[:, g % 2, :], bank[0][:, :]).then_inc(tcopied, 1)

            copy_g(0)
            for k in range(NG + 2):
                if 1 <= k <= NG:
                    copy_pT(k - 1)
                if k < NG:
                    exps(k, (0, 1))
                if k + 1 < NG:
                    copy_g(k + 1)
                if 1 <= k <= NG:
                    copy_yT(k - 1)
                if k < NG:
                    exps(k, (2, 3))
                if k == NG - 1:
                    copy_cT(NG - 3)
                    copy_cT(NG - 2)
                if k == NG:
                    copy_cT(NG - 1)
                    act.wait_ge(kspec_done, 1)
                    copy(flat(kh[:, :, :]), bank[2][:, :])
                    copy(kx[:, 0, :], bank[2][:, BH:2 * BH], scale=-1.0)
                    copy(kx[:, 1, :], bank[2][:, 0:BH]).then_inc(kspec_copied, 1)

            act.wait_ge(top_ready, 1)
            act.activation(ex[:, :], bank[2][:, 0:T], ACT.Exp, bias=nmx[:, 0:1]).then_inc(lag_exp, 1)
            act.wait_ge(theta_ready, 1)
            act.activation(th[:, T_SIN, :], ph[:, P_ANGLE, 0, :], ACT.Sin)
            act.activation(th[:, T_SINH, :], ph[:, P_ANGLE, 0, :], ACT.Sin, scale=0.5).then_inc(sines_done, 1)
            act.wait_ge(weights_ready, 1)
            act.activation(ab[:, A_CS, :], wf[:, 0, :], ACT.Copy,
                           scale=wsm[:, L_SIN:L_SIN + 1]).then_inc(lag_scaled, 1)
            act.wait_ge(z_done, 1)
            act.wait_ge(lag_sum, 1)
            copy(z[:, :], bank[3][:, 0:C], scale=wsm[:, L_SCALE:L_SCALE + 1]).then_inc(z_copied, 1)

            def turns(k):
                act.wait_ge(h_done, k + 1)
                if k >= 2:
                    act.wait_ge(ang_done, k - 1)
                act.activation(turn[:, k % 2, :], bank[HB[k % 4]][:, :], ACT.Identity, scale=0.1 / TWO_PI,
                               bias=ph[:, P_TURN, 1, k % FC:k % FC + 1]).then_inc(turn_done, 1)

            def sine(k):
                act.wait_ge(ang_done, k + 1)
                if k >= 2:
                    act.wait_ge(hid_done, k - 1)
                act.activation(sn[:, k % 2, :], ang[:, k % 2, :], ACT.Sin, scale=TWO_PI * INSIDE,
                               bias=ph[:, P_ANGLE, 1, k % FC:k % FC + 1]).then_inc(sin_done, 1)

            def relu(k):
                act.wait_ge(hid_done, k + 1)
                if k >= NACT:
                    act.wait_ge(down_done, k - NACT + 1)
                act.activation(act_f[:, k % NACT, :], hid[:, k % NHID, :], ACT.Relu,
                               bias=b1_col(k)).then_inc(relu_a_done, 1)

            copy_lnT(0)
            for k in range(NCH + 2):
                if k < NCH:
                    turns(k)
                if 1 <= k <= NCH:
                    sine(k - 1)
                if k % FC == 2 and k // FC + 1 < NG:
                    copy_lnT(k // FC + 1)
                if k >= 2 and (k - 2) % FC != POOL_C:
                    relu(k - 2)

        @block.vector
        def _(dve):
            seq = [0]

            def after(ins):
                seq[0] += 1
                ins.then_inc(dve_seq, 1)
                dve.wait_ge(dve_seq, seq[0])

            def copy(dst, src):
                return dve.tensor_copy(dst, src)

            def batch_stats(g):
                for j in range(G):
                    ins = dve.bn_stats(st[:, g * G + j, :], xs[:, g * G + j, :])
                return ins

            def group_stats(g):
                after(batch_stats(g))
                join_stats(g)

            def join_stats(g):
                for j in range(G):
                    ins = dve.bn_aggr(mv[:, g * G + j, :], st[:, g * G + j, :])
                ins.then_inc(stats, 1)

            def norm0(g):
                dve.wait_ge(scaled, g + 1)
                for j in range(G // 2, G):
                    b = g * G + j
                    ins = dve.tensor_scalar(xn[:, b, 0:C], xs[:, b, :], rstd[:, b:b + 1], shift[:, b:b + 1],
                                            ALU.mult, ALU.add)
                ins.then_inc(normed, 1)

            def copy_lora():
                dve.wait_ge(small_tposed, 1)
                copy(lo_aT[:, :], bank[6][0:RANK, 0:128])
                copy(lp_aT[:, :], bank[6][0:RANK, 128:256]).then_inc(lora_copied, 1)

            def copy_vectors():
                dve.wait_ge(vec_tposed, 1)
                copy(vcol[:, :], bank[6][:, 256:256 + NV]).then_inc(vec_copied, 1)

            def add_lora():
                dve.wait_ge(lora_prod, 1)
                for n in range(3):
                    ins = dve.scalar_tensor_tensor(wa[:, n, :], bank[7][:, n * C:(n + 1) * C], 1.0, wa[:, n, :],
                                                   ALU.mult, ALU.add, accum_out=wsum[:, n:n + 1])
                after(ins)
                dve.tensor_scalar(wsum[:, :], wsum[:, :], -1.0 / C, None, ALU.mult).then_inc(lora_added, 1)

            def phase(i):
                return ph[:, i, :, :]

            def reduce_phases():
                dve.wait_ge(vec_copied, 1)
                copy(ph[:, P_IN, 0, :], vcol[:, V_THETA:V_THETA + FC])
                after(dve.scalar_tensor_tensor(ph[:, P_IN, 1, :], vcol[:, V_B1:V_B1 + FC], 0.1,
                                               vcol[:, V_THETA:V_THETA + FC], ALU.mult, ALU.add))
                after(dve.tensor_scalar(phase(P_ROUND), phase(P_IN), 1.0 / TWO_PI, ROUND, ALU.mult, ALU.add))
                after(dve.tensor_scalar(phase(P_ROUND), phase(P_ROUND), ROUND, None, ALU.subtract))
                after(dve.scalar_tensor_tensor(phase(P_RED), phase(P_ROUND), -PI_A, phase(P_IN), ALU.mult, ALU.add))
                for rest in (PI_B, PI_C):
                    after(dve.scalar_tensor_tensor(phase(P_RED), phase(P_ROUND), -rest, phase(P_RED),
                                                   ALU.mult, ALU.add))
                dve.tensor_scalar(phase(P_TURN), phase(P_RED), 1.0 / TWO_PI, None, ALU.mult)
                dve.tensor_scalar(phase(P_ANGLE), phase(P_RED), INSIDE, None, ALU.mult).then_inc(theta_ready, 1)

            def repeat_b1():
                b1_ = vcol[:, V_B1 + POOL_C:V_B1 + POOL_C + 1]
                dve.tensor_scalar(negb1[:, :], b1_, -1.0, None, ALU.mult)
                dve.tensor_scalar(b1rep[:, :], ones[:, :], b1_, None, ALU.mult).then_inc(b1_repeated, 1)

            def col(i):
                return th[:, i, :]

            def make_kappa():
                wr, wi = vcol[:, V_REAL:V_REAL + FC], vcol[:, V_IMAG:V_IMAG + FC]
                dve.wait_ge(sines_done, 1)
                after(dve.tensor_tensor(col(T_COS), col(T_SINH), col(T_SINH), ALU.mult))
                after(dve.tensor_scalar(col(T_COS), col(T_COS), -2.0, 1.0, ALU.mult, ALU.add))
                after(dve.tensor_tensor(col(T_COS), col(T_COS), wr, ALU.mult))
                after(dve.tensor_tensor(col(T_MIX), col(T_SIN), wi, ALU.mult))
                after(dve.tensor_tensor(col(T_MIX), col(T_MIX), col(T_COS), ALU.add))
                after(dve.tensor_tensor(col(T_MIX), col(T_MIX), wi, ALU.mult))
                after(dve.tensor_scalar(col(T_KAPPA), col(T_MIX), 0.1, None, ALU.mult))

            dve.memset(zeros[:, :], 0.0).then_inc(zeros_set, 1)
            for g in range(NG):
                dve.wait_ge(x_in[g], 16)
                group_stats(g)
                if g >= 1:
                    norm0(g - 1)
                if g == 1:
                    copy_lora()
                if g == 2:
                    add_lora()
                if g == 7:
                    copy_vectors()
                    dve.wait_ge(bias_copied, 1)
                    dve.tensor_tensor(wqc[:, :], wqs[:, :], bc[:, NR:NR + HD], ALU.add).then_inc(wqc_ready, 1)
            norm0(NG - 1)

            dve.wait_ge(tg_done, 1)
            dve.wait_ge(wm_copied, 1)
            copy(mu[:, :], bank[6][:, 0:3 * (C + 1)].rearrange("p (n c) -> p n c", n=3)[:, :, C])
            for n in range(3):
                ins = dve.tensor_tensor_reduce(out=tg[:, n, :], in0=bank[6][:, n * (C + 1):n * (C + 1) + C],
                                               in1=wm[:, n, :], scale=1.0, scalar=0.0, op0=ALU.mult, op1=ALU.add,
                                               accum_out=q2[:, n:n + 1])
            after(ins)
            after(dve.tensor_tensor(bn[:, B_MEAN2, :], mu[:, :], mu[:, :], ALU.mult))
            dve.scalar_tensor_tensor(bn[:, B_VAR, :], q2[:, :], EPS, bn[:, B_MEAN2, :], ALU.add,
                                     ALU.subtract).then_inc(bn_var, 1)
            dve.tensor_scalar(bn[:, B_BETA, :], vcol[:, V_BETA:V_BETA + 3], 1.0 / C, None, ALU.mult)
            after(dve.scalar_tensor_tensor(bn[:, B_GMEAN, :], mu[:, :], -1.0 / C, vcol[:, V_GAMMA:V_GAMMA + 3],
                                           ALU.mult, ALU.mult))
            dve.wait_ge(bn_rstd, 1)
            dve.tensor_tensor(bn[:, B_SCALE, :], bn[:, B_RSTD, :], vcol[:, V_GAMMA:V_GAMMA + 3], ALU.mult)
            after(dve.tensor_tensor(bn[:, B_GMEAN_STD, :], bn[:, B_RSTD, :], bn[:, B_GMEAN, :], ALU.mult))
            dve.tensor_tensor(bn[:, B_SHIFT, :], bn[:, B_GMEAN_STD, :], bn[:, B_BETA, :],
                              ALU.add).then_inc(bn_ready, 1)
            dve.wait_ge(bn_ready, 1)
            for n in range(2):
                ins = dve.tensor_scalar(w3[:, n, :], wm[:, n, :], bn[:, B_SCALE, n:n + 1], bn[:, B_SHIFT, n:n + 1],
                                        ALU.mult, ALU.add)
            ins.then_inc(w3_ready, 1)
            reduce_phases()
            repeat_b1()
            dve.reciprocal(std0[:, :], rstd[:, :])

            bqb = bc[:, R_BQ:R_BQ + HD].unsqueeze(1).broadcast_to([128, B, HD])

            def heads(ap):
                return ap.rearrange("p (b h) -> p b h", h=HD)

            def row_max(g):
                dve.wait_ge(s_done, g + 1)
                dve.tensor_reduce(negmax[:, g * G:(g + 1) * G],
                                  bank[2 + g % 2][:, :].rearrange("p (b t) -> p b t", b=G),
                                  AX.X, ALU.max, negate=True).then_inc(max_done, 1)

            def add_y(g):
                dve.wait_ge(exp_done, (g + 1) * G)
                after(dve.reciprocal(rinv[:, g * G:(g + 1) * G], rowsum[:, g * G:(g + 1) * G]))
                dve.wait_ge(y_done, g + 1)
                for j in range(G):
                    b = g * G + j
                    ins = dve.scalar_tensor_tensor(xs[:, b, :], y_part(j)[:, 0:C], rinv[:, b:b + 1],
                                                   xs[:, b, :], ALU.mult, ALU.add)
                for n in range(2):
                    a = g * G + 2 * n
                    both = bank[YB[n]][:, 0:2 * (C + HD)].rearrange("p (b c) -> p b c", b=2)
                    ins = dve.tensor_tensor(heads(qy[:, :])[:, a:a + 2, :], both[:, :, C:],
                                            rinv[:, a:a + 2].unsqueeze(2).broadcast_to([T, 2, HD]), ALU.mult)
                ins.then_inc(resid, 1)

            def make_kv(part):
                a, b = KPART[part] * G, KPART[part + 1] * G
                dve.wait_ge(k_done, KPART[part + 1])
                dve.tensor_tensor(heads(kv[:, :])[:, a:b, :], heads(bank[5][:, 0:BH])[:, a:b, :], bqb[:, a:b, :],
                                  ALU.add).then_inc(kv_ready, 1)
                dve.wait_ge(kv_ready, part + 1)

            def take_q(part):
                a, b = QPART[part] * G, QPART[part + 1] * G
                dve.wait_ge(q_done, QPART[part + 1])
                dve.tensor_tensor(heads(qx[:, :])[:, a:b, :], heads(bank[5][:, BH:2 * BH])[:, a:b, :],
                                  std0[:, a:b].unsqueeze(2).broadcast_to([T, b - a, HD]),
                                  ALU.mult).then_inc(q_taken, 1)

            def make_q(part):
                a, b = QPART[part], QPART[part + 1]
                cols = slice(a * G * HD, b * G * HD)
                view = heads(q[:, :])[:, a * G:b * G, :]
                dve.wait_ge(q_taken, part + 1)
                dve.wait_ge(resid, b)
                after(dve.tensor_tensor(qy[:, cols], qy[:, cols], qx[:, cols], ALU.add))
                dve.wait_ge(scaled, NG + b)
                after(dve.tensor_tensor(view, heads(qy[:, :])[:, a * G:b * G, :],
                                        rstd[:, a * G:b * G].unsqueeze(2).broadcast_to([T, (b - a) * G, HD]),
                                        ALU.mult))
                dve.tensor_tensor(view, view, bqb[:, a * G:b * G, :], ALU.add).then_inc(q_ready, 1)

            def correlate(part):
                a, b = QPART[part] * G * HD, QPART[part + 1] * G * HD
                spec = bank[SB[part]][:, 0:2 * (b - a)].rearrange("p (s n) -> p s n", s=2)
                dve.wait_ge(qspec_done, part + 1)
                for i, (k_, j_) in enumerate(((kh, junk), (kx, junk2))):
                    ins = dve.tensor_tensor_reduce(
                        out=j_[:, 0:2 * (b - a)].rearrange("p (s n) -> p s n", s=2), in0=spec, in1=k_[:, :, a:b],
                        scale=1.0 / (T * BH), scalar=pw[:, i:i + 1] if part else 0.0, op0=ALU.mult, op1=ALU.add,
                        accum_out=pw[:, 2 * part + i:2 * part + i + 1])
                if part:
                    ins.then_inc(power_ready, 1)
                else:
                    after(ins)

            for k in range(NG + 2):
                if k == NG - 1:
                    take_q(0)
                if 2 <= k:
                    add_y(k - 2)
                if k < NG:
                    row_max(k)
                if k == 1:
                    dve.wait_ge(bias_copied, 1)
                    make_kv(0)
                if 2 <= k:
                    if k - 2 < KPART[1]:
                        repeat_v(dve, k - 2).then_inc(v_repeated, 1)
                    dve.wait_ge(resid, k - 1)
                    group_stats(k - 2)
                if k == NG + 1:
                    make_kv(1)
                    take_q(1)
                if k == NG:
                    make_q(0)

            make_q(1)
            dve.wait_ge(kspec_copied, 1)
            correlate(0)
            correlate(1)
            dve.memset(cw[:, T:T + 8], PADDING)
            dve.wait_ge(b1w2_done, 1)
            dve.tensor_tensor(bc[:, R_B2:R_B2 + C], bank[4][:, 0:C], bc[:, R_B2:R_B2 + C],
                              ALU.add).then_inc(b2_ready, 1)
            dve.wait_ge(corr_done, 1)
            after(dve.max(top[:, 0:8], bank[2][:, 0:T]))
            dve.match_replace(cw[:, 0:T], top[:, 0:8], bank[2][:, 0:T], TAKEN).then_inc(dve_seq, 1)
            seq[0] += 1
            dve.tensor_scalar(nmx[:, :], top[:, 0:1], -1.0, None, ALU.mult).then_inc(top_ready, 1)
            dve.wait_ge(dve_seq, seq[0])
            after(dve.max(top[:, 8:16], cw[:, :]))
            after(dve.memset(top[:, K_TOP:16], PADDING))
            after(dve.match_replace(cw2[:, :], top[:, 8:16], cw[:, :], TAKEN))
            dve.wait_ge(lag_exp, 1)
            after(dve.scalar_tensor_tensor(ew[:, :], cw2[:, 0:T], TAKEN, ex[:, :], ALU.is_equal, ALU.mult,
                                           accum_out=wsm[:, L_SUM:L_SUM + 1]))
            dve.tensor_tensor_reduce(out=junk[:, 0:T], in0=ew[:, :], in1=cosm[:, :], scale=1.0, scalar=0.0,
                                     op0=ALU.mult, op1=ALU.add, accum_out=wsm[:, L_COS:L_COS + 1])
            after(dve.tensor_tensor_reduce(out=junk2[:, 0:T], in0=ew[:, :], in1=sinm[:, :], scale=1.0, scalar=0.0,
                                           op0=ALU.mult, op1=ALU.add, accum_out=wsm[:, L_SIN:L_SIN + 1]))
            dve.sem_inc(weights_ready, 1)
            dve.wait_ge(wf_copied, 1)
            after(dve.tensor_scalar(ab[:, A_SS, :], wf[:, 1, :], wsm[:, L_SIN:L_SIN + 1], None, ALU.mult))
            dve.scalar_tensor_tensor(ab[:, A_COS, :], wf[:, 0, :], wsm[:, L_COS:L_COS + 1], ab[:, A_SS, :],
                                     ALU.mult, ALU.subtract)
            dve.wait_ge(lag_scaled, 1)
            dve.scalar_tensor_tensor(ab[:, A_SIN, :], wf[:, 1, :], wsm[:, L_COS:L_COS + 1], ab[:, A_CS, :],
                                     ALU.mult, ALU.add).then_inc(zspec_ready, 1)
            after(dve.reciprocal(wsm[:, L_INV:L_INV + 1], wsm[:, L_SUM:L_SUM + 1]))
            dve.tensor_scalar(wsm[:, L_SCALE:L_SCALE + 1], wsm[:, L_INV:L_INV + 1], 1.0 / T, None,
                              ALU.mult).then_inc(lag_sum, 1)

            def add_cross(g):
                dve.wait_ge(r_done, g + 1)
                dve.wait_ge(biased, g + 1)
                dve.tensor_tensor(flat(grp(xs, g)), bank[RB[min(g, AHEAD)]][:, :], flat(grp(xs, g)),
                                  ALU.add).then_inc(resid, 1)
                dve.wait_ge(resid, NG + g + 1)

            def angle(k):
                dve.wait_ge(turn_done, k + 1)
                if k >= 2:
                    dve.wait_ge(sin_done, k - 1)
                dve.scalar_tensor_tensor(ang[:, k % 2, :], bank[HB[k % 4]][:, :], 0.1 / TWO_PI, turn[:, k % 2, :],
                                         ALU.mult, ALU.subtract).then_inc(ang_done, 1)

            def hidden(k):
                dve.wait_ge(sin_done, k + 1)
                if k >= NHID:
                    wait_relu(dve, k - NHID)
                c = k % FC
                dve.scalar_tensor_tensor(hid[:, k % NHID, :], sn[:, k % 2, :], th[:, T_KAPPA, c:c + 1],
                                         bank[HB[k % 4]][:, :], ALU.mult, ALU.add).then_inc(hid_done, 1)

            def output(g):
                dve.wait_ge(down_done, (g + 1) * FC)
                dve.wait_ge(biased, NG + g + 1)
                if g >= 2:
                    dve.wait_ge(out_sent[g % 2], 16 * (g // 2))
                for a, b in ((0, G // 2), (G // 2, G)) if g == NG - 1 else ((0, G),):
                    dve.tensor_tensor(flat(outs[:, g % 2, a:b, :]), bank[OB[g % 2]][:, a * C:b * C],
                                      flat(xs[:, g * G + a:g * G + b, :]), ALU.add).then_inc(o_done, 1)

            make_kappa()
            add_cross(0)
            group_stats(0)
            add_cross(1)
            after(batch_stats(1))
            dve.wait_ge(scaled, 2 * NG + 1)
            for b in range(FIRST_DVE):
                dve.tensor_scalar(ln[:, 0, b, :], xs[:, b, :], mv[:, b, 0:1], rstd[:, b:b + 1],
                                  ALU.subtract, ALU.mult).then_inc(first_normed, 1)
            join_stats(1)
            add_cross(2)
            group_stats(2)
            for k in range(NCH + LAG + 2):
                if k < NCH:
                    angle(k)
                if 1 <= k <= NCH:
                    hidden(k - 1)
                if k % FC == 1 and 2 < k // FC + 2 < NG:
                    add_cross(k // FC + 2)
                    group_stats(k // FC + 2)
                if k >= LAG + FC and (k - LAG) % FC == 1:
                    output((k - LAG) // FC - 1)

        @block.tensor
        def _(pe):
            def mm(dst, lhsT, rhs, start=True, stop=True, **kw):
                return pe.matmul(dst, lhsT, rhs, start=start, stop=stop, **kw)

            def tr(dst, src, n=128):
                return pe.transpose(dst, src, ident[0:n, 0:n])

            def small_transposes():
                pe.wait_ge(attn_w_in, 64)
                tr(bank[6][0:RANK, 0:128], lo_a[:, :])
                tr(bank[6][0:RANK, 128:256], lp_a[:, :]).then_inc(small_tposed, 1)

            def vec_transposes():
                pe.wait_ge(vec_in, 96)
                pe.wait_ge(lora_copied, 1)
                tr(bank[6][:, 256:256 + NV], vrow[:, :], NV).then_inc(vec_tposed, 1)

            def lora_product():
                pe.wait_ge(lora_copied, 1)
                mm(bank[7][:, 0:3 * C], lo_aT[:, :], lo_b[:, :]).then_inc(lora_prod, 1)
                pe.wait_ge(proj_w_in, 32)
                mm(bank[3][:, 0:C], lp_b[:, :], lp_aT[:, :], stop=False)
                mm(bank[3][:, 0:C], wp[:, :], ident[:, :], start=False).then_inc(wmpT_done, 1)

            def wm_transposes():
                pe.wait_ge(wm3_ready, 1)
                for n in range(3):
                    ins = tr(bank[7][:, n * C:(n + 1) * C], wm3[:, n, :])
                ins.then_inc(wm3_tposed, 1)

            def wm_back():
                pe.wait_ge(wmT_copied, 1)
                for n in range(3):
                    ins = tr(bank[7][:, n * C:(n + 1) * C], wmT[:, n, :])
                ins.then_inc(wm_tposed, 1)

            def fold_projections():
                pe.wait_ge(wmpT_copied, 1)
                mm(bank[3][:, C:2 * C], wp[:, :], wmpT[:, :])
                mm(bank[3][:, 2 * C:3 * C], wmpT[:, :], wp[:, :]).then_inc(woT_done, 1)

            def spread_biases():
                pe.wait_ge(rows_in, 48)
                pe.wait_ge(wm_copied, 1)
                pe.wait_ge(cross_w_in, 16)
                mm(bank[7][:, 0:NR], ones[0:1, :], rrow[:, :])
                mm(bank[7][:, NR:NR + HD], negmean[:, :], wqs[:, :]).then_inc(bias_spread, 1)

            def ctx_transpose(g):
                pe.wait_ge(c_in[g], 16)
                if g == 0:
                    pe.wait_ge(woT_copied, 1)
                elif 2 <= g < KPART[1]:
                    pe.wait_ge(ct_copied, g - 1)
                elif g == NG - 3:
                    pe.wait_ge(g_copied, NG)
                elif g == NG - 2:
                    pe.wait_ge(exp_done, (NG - 1) * G)
                elif g == NG - 1:
                    pe.wait_ge(exp_done, NG * G)
                for j in range(G):
                    ins = tr(bank[TB[g]][:, j * T:(j + 1) * T], cs[:, g * G + j, :])
                ins.then_inc(ct_done, 1)

            def ctx_k(g):
                if g == 0:
                    pe.wait_ge(cross_w_in, 16)
                pe.wait_ge(ct_copied, g + 1)
                for j in range(G):
                    b = g * G + j
                    ins = mm(bank[5][:, b * HD:(b + 1) * HD], cT[:, g % 2, j * T:(j + 1) * T], wqs[:, :])
                ins.then_inc(k_done, 1)

            def keep_busy(bank_, n):
                for _ in range(n):
                    mm(bank_[:, :], zeros[:, 0:128], zeros[:, :])

            pe.wait_ge(zeros_set, 1)
            keep_busy(bank[5], WARM_UP)
            pe.wait_ge(consts_set, 5)
            small_transposes()
            for g in range(NG):
                pe.wait_ge(normed, g + 1)
                pe.wait_ge(normed_a, g + 1)
                if g >= 2:
                    pe.wait_ge(tcopied, g - 1)
                for j in range(G):
                    ins = tr(bank[1 + g % 2][:, j * T:(j + 1) * T], xn[:, g * G + j, 0:C])
                ins.then_inc(tposed, 1)
                for j in range(G):
                    b = g * G + j
                    ins = mm(bank[0][:, 0:C + 1], xn[:, b, 0:C], xn[:, b, :], start=b == 0, stop=b == B - 1)
                if g == NG - 1:
                    ins.then_inc(gram_done, 1)
                if g == 0:
                    lora_product()
                if g == 3:
                    fold_projections()
                    wm_transposes()
                if g == 4:
                    wm_back()
                if g == 5:
                    spread_biases()
                    vec_transposes()
                    ctx_transpose(0)
            ctx_transpose(1)
            pe.wait_ge(gram_copied, 1)
            pe.wait_ge(wmT_copied, 1)
            pe.wait_ge(vec_copied, 1)
            for n in range(3):
                ins = mm(bank[6][:, n * (C + 1):(n + 1) * (C + 1)], wmT[:, n, :], gram[:, :])
            ins.then_inc(tg_done, 1)
            pe.wait_ge(wqc_ready, 1)
            mm(bank[0][:, 0:HD], wox[:, 1, 0:C], wqc[:, :]).then_inc(woq_done, 1)
            pe.wait_ge(dft_in, 48)
            pe.wait_ge(wmT_copied, 1)
            mm(bank[7][:, 0:C], cosm[:, :], wouts[:, :])
            mm(bank[7][:, C:2 * C], sinm[:, :], wouts[:, :]).then_inc(wf_done, 1)
            for g in (1, 2):
                ctx_k(g - 1)
                ctx_transpose(g + 1)
            ctx_k(2)
            pe.wait_ge(woq_copied, 1)
            keep_busy(bank[0], 1)
            pe.wait_ge(w3_ready, 1)
            mm(bank[6][:, 0:C], w3[:, 0, :], w3[:, 1, :])
            pe.wait_ge(w3v_ready, 1)
            mm(bank[6][:, C:2 * C + HD], w3[:, 2, :], wox[:, 0, :]).then_inc(mqk_done, 1)
            def scores_left(g):
                if g == 0:
                    pe.wait_ge(mqk_copied, 1)
                    pe.wait_ge(tcopied, NG)
                else:
                    pe.wait_ge(g_copied, g)
                mm(bank[1][:, :], mqk[:, :], flat(grp(xnT, g))).then_inc(g_done, 1)

            def mask(g):
                if g >= 2:
                    pe.wait_ge(exp_done, (g - 1) * G)
                elif g == 1:
                    pe.wait_ge(ct_copied, KPART[1])
                mm(bank[2 + g % 2][:, :].rearrange("p (b t) -> p b t", b=G), identb[:, :],
                   maskb[:, :].unsqueeze(1).broadcast_to([T, G, T]), stop=False, skip_group_check=True)

            def scores(g):
                pe.wait_ge(g_copied, g + 1)
                for j in range(G):
                    ins = mm(bank[2 + g % 2][:, j * T:(j + 1) * T], gT[:, g % 2, j * T:(j + 1) * T],
                             xnT[:, g * G + j, :], start=False, stop=j == G - 1, skip_group_check=True)
                ins.then_inc(s_done, 1)

            def p_transpose(g):
                pe.wait_ge(exp_done, (g + 1) * G)
                if g == 0:
                    pe.wait_ge(ct_copied, KPART[1] - 1)
                else:
                    pe.wait_ge(pt_copied, g)
                for j in range(G):
                    ins = tr(bank[4][:, j * T:(j + 1) * T], p[:, g % 2, j, :])
                ins.then_inc(pt_done, 1)

            def weigh(g):
                pe.wait_ge(pt_copied, g + 1)
                if g == 0:
                    pe.wait_ge(wvo_copied, 1)
                else:
                    pe.wait_ge(yt_copied, g)
                for j in range(G):
                    ins = mm(bank[6][:, j * T:(j + 1) * T], xn[:, g * G + j, 0:C], pT[:, g % 2, j * T:(j + 1) * T])
                ins.then_inc(yt_done, 1)

            def project(g):
                pe.wait_ge(yt_copied, g + 1)
                if g == 0:
                    pe.wait_ge(wf_copied, 1)
                else:
                    pe.wait_ge(resid, g)
                for j in range(G):
                    ins = mm(y_part(j), yT[:, g % 2, j * T:(j + 1) * T], wvo[:, :])
                ins.then_inc(y_done, 1)

            def ln_transpose(g):
                if g == 0:
                    pe.wait_ge(resid, NG)
                else:
                    pe.wait_ge(tcopied, NG + g)
                    pe.wait_ge(normed, NG + g + 1)
                for j in range(G):
                    if g == 0 and j < FIRST_DVE:
                        pe.wait_ge(first_normed, j + 1)
                    elif g == 0:
                        pe.wait_ge(normed, NG + 1)
                    ins = tr(bank[0][:, j * T:(j + 1) * T], ln[:, g % 2, j, :])
                ins.then_inc(tposed, 1)

            def cross_q(g):
                if g == 0:
                    pe.wait_ge(kv_ready, 1)
                    pe.wait_ge(wqc_ready, 1)
                elif g == QPART[1]:
                    pe.wait_ge(q_taken, 1)
                for j in range(G):
                    b = g * G + j
                    ins = mm(bank[5][:, BH + b * HD:BH + (b + 1) * HD], xnT[:, b, :], wqc[:, :])
                ins.then_inc(q_done, 1)

            def query_spectrum(part):
                a, b = QPART[part] * G * HD, QPART[part + 1] * G * HD
                pe.wait_ge(q_ready, part + 1)
                if part == 0:
                    pe.wait_ge(ct_copied, NG)
                else:
                    pe.wait_ge(ct_copied, NG - 2)
                mm(bank[SB[part]][:, 0:b - a], cosm[:, :], q[:, a:b])
                mm(bank[SB[part]][:, b - a:2 * (b - a)], sinm[:, :], q[:, a:b]).then_inc(qspec_done, 1)

            def key_spectrum(part):
                a, b = KPART[part] * G * HD, KPART[part + 1] * G * HD
                pe.wait_ge(kv_ready, part + 1)
                if part == 0:
                    pe.wait_ge(ct_copied, NG - 1)
                mm(bank[2][:, a:b], cosm[:, :], kv[:, a:b])
                ins = mm(bank[2][:, BH + a:BH + b], sinm[:, :], kv[:, a:b])
                if part:
                    ins.then_inc(kspec_done, 1)

            ctx_transpose(NG - 4)
            ctx_k(NG - 5)
            scores_left(0)
            ctx_k(NG - 4)
            mask(0)
            for k in range(NG + 1):
                if k == 1:
                    mask(1)
                if k < NG:
                    scores(k)
                if 1 <= k <= NG:
                    p_transpose(k - 1)
                if k + 1 < NG:
                    scores_left(k + 1)
                elif k + 1 == NG:
                    ctx_transpose(NG - 3)
                    ctx_transpose(NG - 2)
                elif k == NG:
                    ctx_transpose(NG - 1)
                    ctx_k(NG - 3)
                if 1 <= k <= NG:
                    weigh(k - 1)
                    cross_q(k - 1)
                    if k + 1 < NG:
                        mask(k + 1)
                    project(k - 1)
            ctx_k(NG - 2)
            ctx_k(NG - 1)
            key_spectrum(0)
            query_spectrum(0)
            key_spectrum(1)
            keep_busy(bank[1], 6)

            pe.wait_ge(w2_in, 16)
            pe.wait_ge(b1_repeated, 1)
            mm(bank[4][:, 0:C], b1rep[:, :], w2s[:, POOL_C, :]).then_inc(b1w2_done, 1)
            query_spectrum(1)
            keep_busy(bank[6], 5)
            pe.wait_ge(power_ready, 1)
            pe.wait_ge(kspec_copied, 1)
            mm(bank[2][:, 0:T], pw[:, 2:3].broadcast_to([T, T]), cosm[:, :], stop=False)
            mm(bank[2][:, 0:T], pw[:, 3:4].broadcast_to([T, T]), sinm[:, :], start=False).then_inc(corr_done, 1)
            keep_busy(bank[0], 13)
            pe.wait_ge(zspec_ready, 1)
            mm(bank[3][:, 0:C], cosm[:, :], ab[:, A_COS, :], stop=False)
            mm(bank[3][:, 0:C], sinm[:, :], ab[:, A_SIN, :], start=False).then_inc(z_done, 1)

            keep_busy(bank[0], 2)

            def cross_out(g):
                pe.wait_ge(z_copied, 1)
                if g < KPART[1]:
                    pe.wait_ge(v_repeated, g + 1)
                else:
                    pe.wait_ge(v_repeated_p, g + 1 - KPART[1])
                if g == 0:
                    pe.wait_ge(b2_ready, 1)
                elif g >= AHEAD:
                    pe.wait_ge(resid, NG + (1 if g == AHEAD else g))
                for j in range(G):
                    ins = mm(bank[RB[min(g, AHEAD)]][:, j * C:(j + 1) * C], cs[:, g * G + j, :], z[:, :])
                ins.then_inc(r_done, 1)

            def up(k):
                g, c = divmod(k, FC)
                pe.wait_ge(tcopied, NG + g + 1)
                if k >= 4:
                    pe.wait_ge(hid_done, k - 3)
                if k == 0:
                    pe.wait_ge(w1_in, 16)
                mm(bank[HB[k % 4]][:, :], w1s[:, c * 128:(c + 1) * 128], lnT[:, g % 2, :]).then_inc(h_done, 1)

            def down(k):
                g, c = divmod(k, FC)
                wait_relu(pe, k)
                if k == 0:
                    pe.wait_ge(w2_in, 16)
                if c == 0:
                    if g >= 2:
                        pe.wait_ge(o_done, g - 1)
                    else:
                        pe.wait_ge(resid, NG + g + 2)
                for j in range(G):
                    ins = mm(bank[OB[g % 2]][:, j * C:(j + 1) * C], act_f[:, k % NACT, j * T:(j + 1) * T],
                             w2s[:, c, :], start=c == 0 and j == 0, stop=c == FC - 1 and j == G - 1,
                             skip_group_check=True)
                ins.then_inc(down_done, 1)

            for g in range(AHEAD + 1):
                cross_out(g)
            keep_busy(bank[2], 7)
            ln_transpose(0)
            for k in range(NCH + LAG):
                g, c = divmod(k, FC)
                if k < NCH:
                    up(k)
                if c == 3 and AHEAD < g + 3 < NG:
                    cross_out(g + 3)
                if c == (3 if g == 0 else 2) and g + 1 < NG:
                    ln_transpose(g + 1)
                if k >= LAG:
                    down(k - LAG)


_INS = ["x", "ctx_1024", "L0_attn_W_attn", "L0_attn_W_proj", "L0_attn_lora_attn_A", "L0_attn_lora_attn_B",
        "L0_attn_lora_proj_A", "L0_attn_lora_proj_B", "L0_attn_bn_gamma", "L0_attn_bn_beta", "L0_xattn_Wq",
        "L0_xattn_bq", "L0_xattn_Wout", "L0_xattn_bout", "L0_ffn_W1", "L0_ffn_b1", "L0_ffn_quantum_phases",
        "L0_ffn_quantum_weights_real", "L0_ffn_quantum_weights_imag", "L0_ffn_W2", "L0_ffn_b2"]


def kernel(**inputs):
    import concourse.bacc as bacc
    from concourse.bass_utils import run_bass_kernel_spmd

    nc = bacc.Bacc("TRN2", target_bir_lowering=False, num_devices=1)
    arrays, args = {}, []
    turns = np.outer(np.arange(T), np.arange(T)) % T * (TWO_PI / T)
    tables = {"dft_cos": np.cos(turns).astype(np.float32), "dft_sin": np.sin(turns).astype(np.float32)}
    for name in [*_INS, *tables]:
        a = np.ascontiguousarray(tables[name] if name in tables else inputs[name])
        arrays[f"in_{name}_dram"] = a
        args.append(nc.dram_tensor(f"in_{name}_dram", a.shape, mybir.dt.from_np(a.dtype),
                                   kind="ExternalInput").ap())
    args.append(nc.dram_tensor("out_0_dram", (B, T, C), FP32, kind="ExternalOutput").ap())
    decoder_layer(nc, *args)
    r = run_bass_kernel_spmd(nc, [arrays], core_ids=[0])
    return r.results[0]["out_0_dram"]
```
